# Optimizing a Trainium2 kernel written in Bass

```python
import numpy as np
import jax
import jax.numpy as jnp

def _softmax(x, axis=-1):
    return jax.nn.softmax(x, axis=axis)

def _gelu(x):
    return jax.nn.gelu(x, approximate=True)

def _silu(x):
    return jax.nn.silu(x)

def _sigmoid(x):
    return jax.nn.sigmoid(x)

def _layernorm(x, axis=-1, eps=1e-05):
    m = jnp.mean(x, axis=axis, keepdims=True)
    v = jnp.var(x, axis=axis, keepdims=True)
    return (x - m) / jnp.sqrt(v + eps)

def _scatter_add(tgt, idx, src, axis=0):
    return tgt.at[idx].add(src)

def _segment_sum(src, seg, n):
    return jax.ops.segment_sum(src, seg, n)
kernel_name = 'mk_seq_preln_d1_jaxref_r8_932339'

def setup_inputs(seed: int=0):
    np.random.seed(seed)
    _w = jnp.asarray

    def _L0_attn_setup():
        import jax, jax.numpy as jnp
        import numpy as np
        B, N, D_IN, D_OUT = (4, 256, 128, 128)
        key = jax.random.key(seed)
        k = jax.random.split(key, 6)
        x = jax.random.normal(k[0], (B, N, D_IN), dtype=jnp.float32)
        sc_in = 1.0 / np.sqrt(D_IN)
        sc_out = 1.0 / np.sqrt(D_OUT)
        W_spin = jax.random.uniform(k[1], (D_OUT, D_IN), jnp.float32, -sc_in, sc_in)
        b_spin = jax.random.uniform(k[2], (D_OUT,), jnp.float32, -sc_in, sc_in)
        W_global = jax.random.uniform(k[3], (D_OUT, D_OUT), jnp.float32, -sc_out, sc_out)
        W_J = jax.random.uniform(k[4], (D_OUT, D_OUT), jnp.float32, -sc_out, sc_out)
        beta = jnp.ones((1,), dtype=jnp.float32)
        return {'x': x, 'W_spin': W_spin, 'b_spin': b_spin, 'W_global': W_global, 'W_J': W_J, 'beta': beta}
    _L0_attn_in = _L0_attn_setup()

    def _L0_ffn_setup():
        import jax, jax.numpy as jnp
        import numpy as np
        E, K, D, H = (8, 2, 128, 256)
        B, S = (1, 128)

        def _grouped_swiglu(x_sorted, counts, w1, w2, w3):
            if hasattr(jax.lax, 'ragged_dot'):
                gs = counts.astype(jnp.int32)
                h = jax.nn.silu(jax.lax.ragged_dot(x_sorted, w1, gs)) * jax.lax.ragged_dot(x_sorted, w3, gs)
                return jax.lax.ragged_dot(h, w2, gs)
            pos = jnp.arange(x_sorted.shape[0])
            eid = jnp.searchsorted(jnp.cumsum(counts), pos, side='right')
            out = jnp.zeros((x_sorted.shape[0], w2.shape[-1]), x_sorted.dtype)
            for e in range(w1.shape[0]):
                xm = jnp.where((eid == e)[:, None], x_sorted, 0.0)
                he = jax.nn.silu(xm @ w1[e]) * (xm @ w3[e])
                out = out + he @ w2[e]
            return out
        key = jax.random.key(seed)
        k0, k1, k2, k3, k4 = jax.random.split(key, 5)
        sD = 1.0 / np.sqrt(D)
        sH = 1.0 / np.sqrt(H)
        return {'hidden_states': jax.random.normal(k0, (B, S, D), jnp.float32), 'gate_w': jax.random.normal(k1, (E, D), jnp.float32) * sD, 'w1': jax.random.normal(k2, (E, D, H), jnp.float32) * sD, 'w2': jax.random.normal(k3, (E, H, D), jnp.float32) * sH, 'w3': jax.random.normal(k4, (E, D, H), jnp.float32) * sD}
    _L0_ffn_in = _L0_ffn_setup()
    _d = {'L0_attn_x': _L0_attn_in['x'], 'L0_attn_W_spin': _L0_attn_in['W_spin'], 'L0_attn_b_spin': _L0_attn_in['b_spin'], 'L0_attn_W_global': _L0_attn_in['W_global'], 'L0_attn_W_J': _L0_attn_in['W_J'], 'L0_attn_beta': _L0_attn_in['beta'], 'L0_ffn_gate_w': _L0_ffn_in['gate_w'], 'L0_ffn_w1': _L0_ffn_in['w1'], 'L0_ffn_w2': _L0_ffn_in['w2'], 'L0_ffn_w3': _L0_ffn_in['w3']}
    _x0 = _d['L0_attn_x']
    _d['L0_attn_x'] = jax.random.normal(jax.random.fold_in(jax.random.key(seed), 1), (2, 1024, 128), dtype=_x0.dtype)
    del _x0
    return _d

def reference(L0_attn_x, L0_attn_W_spin, L0_attn_b_spin, L0_attn_W_global, L0_attn_W_J, L0_attn_beta, L0_ffn_gate_w, L0_ffn_w1, L0_ffn_w2, L0_ffn_w3):

    def _L0_attn_ref(x, W_spin, b_spin, W_global, W_J, beta):
        import jax, jax.numpy as jnp
        import numpy as np
        B, N, D_IN, D_OUT = (4, 256, 128, 128)
        s = jnp.einsum('bni,oi->bno', x, W_spin) + b_spin
        mean_field = jnp.mean(s, axis=1, keepdims=True)
        global_influence = jnp.einsum('bmd,od->bmo', mean_field, W_global)
        energy_fields = jnp.einsum('bnd,od->bno', s, W_J)
        scale = 1.0 / jnp.sqrt(jnp.float32(s.shape[2]))
        scores = jnp.einsum('bnd,bmd->bnm', energy_fields, s) * scale
        affinities = jax.nn.softmax(scores, axis=-1)
        local_field = jnp.einsum('bnm,bmd->bnd', affinities, s)
        return jnp.tanh(beta * (s + global_influence + local_field))

    def _L0_ffn_ref(hidden_states, gate_w, w1, w2, w3):
        import jax, jax.numpy as jnp
        import numpy as np
        E, K, D, H = (8, 2, 128, 256)
        B, S = (1, 128)

        def _grouped_swiglu(x_sorted, counts, w1, w2, w3):
            if hasattr(jax.lax, 'ragged_dot'):
                gs = counts.astype(jnp.int32)
                h = jax.nn.silu(jax.lax.ragged_dot(x_sorted, w1, gs)) * jax.lax.ragged_dot(x_sorted, w3, gs)
                return jax.lax.ragged_dot(h, w2, gs)
            pos = jnp.arange(x_sorted.shape[0])
            eid = jnp.searchsorted(jnp.cumsum(counts), pos, side='right')
            out = jnp.zeros((x_sorted.shape[0], w2.shape[-1]), x_sorted.dtype)
            for e in range(w1.shape[0]):
                xm = jnp.where((eid == e)[:, None], x_sorted, 0.0)
                he = jax.nn.silu(xm @ w1[e]) * (xm @ w3[e])
                out = out + he @ w2[e]
            return out
        x = hidden_states.reshape(-1, D)
        N = x.shape[0]
        scores = jax.nn.softmax(x @ gate_w.T, axis=-1)
        top_scores, sel = jax.lax.top_k(scores, K)
        sel_flat = sel.T.reshape(-1)
        scores_flat = top_scores.T.reshape(-1)
        order = jnp.argsort(sel_flat, stable=True)
        tok_sorted = order % N
        scores_sorted = scores_flat[order]
        counts = jnp.bincount(sel_flat, length=E)
        x_sorted = x[tok_sorted]
        y = _grouped_swiglu(x_sorted, counts, w1, w2, w3)
        weighted = y * scores_sorted[:, None]
        out = jnp.zeros((N, D), x.dtype).at[tok_sorted].add(weighted)
        return out.reshape(hidden_states.shape)
    x = L0_attn_x
    x = x + _L0_attn_ref(_layernorm(x, axis=-1), L0_attn_W_spin, L0_attn_b_spin, L0_attn_W_global, L0_attn_W_J, L0_attn_beta)
    x = x + _L0_ffn_ref(_layernorm(x, axis=-1), L0_ffn_gate_w, L0_ffn_w1, L0_ffn_w2, L0_ffn_w3)
    return x

_drawn_inputs = setup_inputs


def setup_inputs(seed=0):
    import zlib

    import numpy as np

    out = dict(_drawn_inputs(seed))
    spreads = {}
    factors = {'L0_attn_W_J': 3.144}
    for name, (base, spread) in spreads.items():
        noise = np.random.default_rng([zlib.crc32(name.encode()), seed]).standard_normal(out[name].shape)
        drawn = base * np.exp(spread * noise) if base else spread * noise
        out[name] = jnp.asarray(drawn.astype(out[name].dtype))
    for name, factor in factors.items():
        out[name] = (out[name] * factor).astype(out[name].dtype)
    return out
```

```python
from contextlib import ExitStack

import numpy as np

import concourse.bass as bass
from concourse import mybir

ALU = mybir.AluOpType
ACT = mybir.ActivationFunctionType
AXX = mybir.AxisListType.X
F32 = mybir.dt.float32
F32R = mybir.dt.float32r
BF16 = mybir.dt.bfloat16
U32 = mybir.dt.uint32
I32 = mybir.dt.int32

P = 128
D = 128
E = 8
H = 256
K = 2
NB = 2
N = 1024
NT = N // P
TILES = NB * NT
GT = 4
GW = GT * P
GROUPS = TILES // GT
GB = NT // GT
CH = N // P
EPS = 1e-5
SCALE = float(D) ** -0.5
QUAD = 4
ST = -(-(K * N // P + E - 1) // QUAD) * QUAD
SLOT_TILES = NB * ST
PAIRS = ST // 2

W_SPIN, W_J, W_GLOB, B_ROW, W_GATE, B_COL, BETA, W_COLS = 0, 128, 256, 384, 512, 520, 521, 522
C_ID, C_TRI, C_ONE, C_DESC, C_THR, C_LT, C_J, C_COLS = 0, 128, 256, 384, 392, 400, 464, 464 + ST


def constants():
    c = np.zeros((P, C_COLS), np.float32)
    c[:, C_ID:C_ID + P] = np.eye(P)
    c[:, C_TRI:C_TRI + P] = np.triu(np.ones((P, P)), 1)
    c[:, C_ONE:C_ONE + P] = 1.0
    c[:, C_DESC:C_DESC + E] = np.arange(E, 0, -1)
    c[:, C_THR:C_THR + N // P] = np.arange(N // P) * P
    c[:, C_LT:C_LT + E * E] = np.tril(np.ones((E, E)), -1).reshape(-1)
    c[:, C_J:C_J + ST] = np.arange(ST)
    return c


def misc_order():
    order = [("xT", 0), ("sT", 0), ("xT", 1), ("sT", 1), ("e", 0), ("V", 0), ("V", 1), ("G", 0)]
    for i in range(TILES):
        g, r = divmod(i, GT)
        if r == 3 and g > 0:
            order.append(("X2", g - 1))
        if i in (0, 1):
            order += [("xT", 2 + i), ("sT", 2 + i)]
        if i == 2:
            order += [("V", 2), ("V", 3), ("G", 1)]
        if r == 1 and g + 1 < GROUPS:
            order.append(("e", g + 1))
        if r == 0 and g > 0:
            order.append(("AV", g - 1))
        if r == 0 and g == 3:
            order.append(("R", 0))
        if r == 1 and g > 0:
            order.append(("OT", g - 1))
        if r == 3 and g > 0:
            order.append(("LG", g - 1))
    last = GROUPS - 1
    return order + [("AV", last), ("OT", last), ("X2", last), ("LG", last), ("R", 1)]


MISC = {use: n for n, use in enumerate(misc_order())}


def build(nc, x, wpack, cst, w13, w2, xs, ys, out):
    ctx = ExitStack()
    with ctx:
        def sb(name, shape, dt=F32):
            return ctx.enter_context(nc.sbuf_tensor(name, shape, dt))

        def sem(name):
            return ctx.enter_context(nc.semaphore(name))

        xt = sb("x_tokens", [P, TILES, D])
        xn = sb("x_normed", [P, TILES, D])
        xnT = sb("x_normed_T", [P, TILES * P])
        sT_hi = sb("sT_hi", [P, TILES * P], F32R)
        sT_lo = sb("sT_lo", [P, TILES * P], F32R)
        e_hi = sb("e_hi", [P, 2, GW], F32R)
        e_lo = sb("e_lo", [P, 2, GW], F32R)
        st = sb("s_tokens", [P, TILES, D])
        v_hi = sb("v_hi", [P, TILES, D], F32R)
        v_lo = sb("v_lo", [P, TILES, D], F32R)
        probs = sb("probs", [P, 2, N])
        pT_hi = sb("pT_hi", [P, 2, CH, GW], F32R)
        pT_lo = sb("pT_lo", [P, 2, CH, GW], F32R)
        arg = sb("tanh_arg", [P, 2, GT, D])
        w = sb("w_packed", [P, W_COLS])
        c = sb("constants", [P, C_COLS])
        tri = sb("tri_bf", [P, P], BF16)
        ones = sb("ones_bf", [P, P], BF16)
        wj_hi = sb("wj_hi", [P, D], F32R)
        wj_lo = sb("wj_lo", [P, D], F32R)
        stage = sb("w13_stage", [P, 2, 2 * H])
        w13_hi = sb("w13_hi", [P, E, 2 * H], F32R)
        w13_lo = sb("w13_lo", [P, E, 2 * H], F32R)
        w2s = sb("w2_rows", [P, E, 2, D])
        zero = sb("zero", [P, D])
        bn = sb("bn_stats", [P, 2, GT, 6])
        mv = sb("mean_var", [P, 2 * TILES, 2])
        rstd = sb("rstd", [P, 2 * TILES])
        veps = sb("var_eps", [P, 2 * TILES])
        mhalf = sb("minus_half", [P, GT])
        ssum = sb("s_sums", [P, GROUPS])
        msum = sb("s_sum", [P, 1])
        meanb = sb("mean_bcast", [P, P])
        gb = sb("global_influence", [P, NB, D])
        nmax = sb("neg_max", [P, TILES])
        L = sb("exp_sums", [P, TILES])
        rL = sb("exp_sums_inv", [P, TILES])
        lg = sb("logits", [P, TILES, E])
        r8 = sb("route_cols", [P, 6, NT])
        r64 = sb("route_rows", [P, 6, NT, E])
        scores = sb("gate_scores", [P, NT, E])
        hot = sb("chosen", [P, K, NT, E])
        sel = sb("selected_bf", [P, NT, E], BF16)
        gate = sb("gate_values", [P, TILES, K])
        cmp = sb("compare", [P, E, E])
        cmpj = sb("compare_tiles", [1, ST, E])
        tiles_e = sb("tiles_of_expert", [P, E])
        base = sb("first_tile", [P, E])
        ends = sb("end_tile", [P, E])
        slotf = sb("slots_f", [P, K, NT])
        slots = sb("slots", [P, NB, K, NT], U32)
        tabf = sb("tile_expert_f", [1, ST])
        tab = sb("tile_expert", [1, SLOT_TILES], I32)
        xs_in = sb("slot_rows", [P, 4, D])

        oT = xnT[:, 0:GW]
        x2T = xnT[:, GW:2 * GW]
        sg = xnT[:, 2 * GW:2 * GW + 2 * H].rearrange("p (u n) -> p u n", u=2)
        h = xnT[:, 3 * GW:3 * GW + 2 * H].rearrange("p (u n) -> p u n", u=2)
        gT_hi = e_hi[:, :, 0:P]
        gT_lo = e_lo[:, :, 0:P]
        hT = probs[:, 0, 0:2 * H].rearrange("p (u n) -> p u n", u=2)
        y = probs[:, 1, 0:4 * D].rearrange("p (v n) -> p v n", v=4)

        ident = c[:, C_ID:C_ID + P]

        S = ctx.enter_context(nc.psum_tensor("S", [P, 2, N], F32))
        PT = ctx.enter_context(nc.psum_tensor("PT", [P, 2, GW], F32))
        MI = ctx.enter_context(nc.psum_tensor("MI", [P, 2, GW], F32))

        x_in = [sem(f"x_in{q}") for q in range(3)]
        w_in = sem("w_in")
        c_in = sem("c_in")
        w2_in = sem("w2_in")
        w13_in = [sem(f"w13_in{k}") for k in range(2)]
        w13_split = sem("w13_split")
        consts_ready = sem("consts_ready")
        wj_ready = sem("wj_ready")
        zero_ready = sem("zero_ready")
        xs_zeroed = [sem(f"xs_zeroed{b}") for b in range(NB)]
        mv_ready = sem("mv_ready")
        rstd_ready = sem("rstd_ready")
        xn_ready = sem("xn_ready")
        misc_full = sem("misc_full")
        misc_free = [sem("misc_free0"), sem("misc_free1")]
        sT_hi_ready = sem("sT_hi_ready")
        e_hi_ready = sem("e_hi_ready")
        mean_ready = sem("mean_ready")
        v_ready = sem("v_ready")
        sg_ready = sem("sG_ready")
        S_full = sem("S_full")
        max_ready = sem("max_ready")
        probs_ready = sem("probs_ready")
        PT_full = sem("PT_full")
        pT_hi_ready = sem("pT_hi_ready")
        pT_ready = sem("pT_ready")
        tanh_ready = sem("tanh_ready")
        x1_ready = sem("x1_ready")
        gate_sub = sem("gate_sub")
        gate_exp = sem("gate_exp")
        sel_ready = sem("sel_ready")
        slots_ready = sem("slots_ready")
        scattered = [sem(f"scattered{b}") for b in range(NB)]
        dve_step = sem("dve_step")
        pool_step = sem("pool_step")
        slot_loaded = [sem(f"slot_loaded{k}") for k in range(2)]
        slotT_full = sem("slotT_full")
        slotT_hi_ready = sem("slotT_hi_ready")
        slotT_ready = sem("slotT_ready")
        gu_full = sem("gu_full")
        silu_ready = sem("silu_ready")
        h_ready = sem("h_ready")
        hT_full = sem("hT_full")
        hT_ready = sem("hT_ready")
        y_full = sem("y_full")
        y_ready = sem("y_ready")
        y_stored = [sem(f"y_stored{k}") for k in range(2)]
        gathered = [sem(f"gathered{t}") for t in range(NT)]
        out_ready = sem("out_ready")
        out_done = sem("out_done")

        def grp(g):
            return slice(g * GT, (g + 1) * GT)

        def cols(g):
            return slice(g * GW, (g + 1) * GW)

        def misc(use):
            return MI[:, MISC[use] % 2, :]

        def bank_free(use):
            return misc_free[MISC[use] % 2]

        def drained(eng, use):
            eng.wait_ge(bank_free(use), MISC[use] // 2 + 1)

        def wait_misc(eng, use):
            eng.wait_ge(misc_full, MISC[use] + 1)

        xg = [x[0, :, :].rearrange("(p t) d -> p t d", t=NT)[:, 0:GT, :],
              x[0, :, :].rearrange("(p t) d -> p t d", t=NT)[:, GT:NT, :],
              x[1, :, :].rearrange("(p t) d -> p t d", t=NT)]
        out_v = out.rearrange("b (p t) d -> p b t d", t=NT)
        xs_pairs = [a.rearrange("(n u p) d -> n p u d", u=2, p=P) for a in xs]
        ys_pairs = [a.rearrange("(n u p) d -> n p u d", u=2, p=P) for a in ys]

        block = ctx.enter_context(nc.Block())

        @block.sync
        def _(sp):
            sp.dma_start(xt[:, 0:GT, :], xg[0]).then_inc(x_in[0], 16)
            sp.dma_start(xt[:, GT:NT, :], xg[1]).then_inc(x_in[1], 16)
            sp.dma_start(xt[:, NT:TILES, :], xg[2]).then_inc(x_in[2], 16)
            for e in range(E):
                if e >= 2:
                    sp.wait_ge(w13_split, e - 1)
                sp.dma_start(stage[:, e % 2, :], w13[:, e, :]).then_inc(w13_in[e % 2], 16)
                if e == 1:
                    sp.dma_start(w2s[:], w2).then_inc(w2_in, 16)
                    sp.wait_ge(zero_ready, 1)
                    for b in range(NB):
                        sp.dma_start(xs[b].rearrange("(n p) d -> p n d", p=P),
                                     zero[:].unsqueeze(1).to_broadcast([P, ST, D])).then_inc(xs_zeroed[b], 16)

            def load_pair(b, k, par):
                sp.dma_start(xs_in[:, 2 * par:2 * par + 2, :], xs_pairs[b][k]).then_inc(slot_loaded[par], 16)

            def store_pair(b, k, par):
                sp.wait_ge(y_ready, 2 * (b * PAIRS + k) + 2)
                sp.dma_start(ys_pairs[b][k], y[:, 2 * par:2 * par + 2, :]).then_inc(y_stored[par], 16)

            def place_free(b, k):
                sp.wait_ge(slotT_full, 2 * (b * PAIRS + k) - 2)

            for b in range(NB):
                sp.wait_ge(scattered[b], 16 * K * NT)
                for u in range(2):
                    if b > 0:
                        place_free(b, u)
                    load_pair(b, u, u)
                    if b > 0:
                        store_pair(b - 1, PAIRS - 2 + u, u)
                with sp.Fori(1, PAIRS // 2) as r:
                    for u in range(2):
                        place_free(b, 2 * r + u)
                        load_pair(b, 2 * r + u, u)
                        store_pair(b, 2 * r + u - 2, u)
            for u in range(2):
                store_pair(NB - 1, PAIRS - 2 + u, u)
            for b in range(NB):
                for t in range(0, NT, 2):
                    sp.wait_ge(out_ready, b * NT + t + 2)
                    sp.dma_start(out_v[:, b, t:t + 2, :], xt[:, b * NT + t:b * NT + t + 2, :]).then_inc(out_done, 16)
            sp.wait_ge(out_done, 16 * NB * NT // 2)

        @block.gpsimd
        def _(pool):
            steps = [0]

            def link(ins):
                steps[0] += 1
                ins.then_inc(pool_step, 1)
                pool.wait_ge(pool_step, steps[0])

            nc.gpsimd.memset(zero[:], 0.0).then_inc(zero_ready, 1)
            link(nc.gpsimd.memset(mhalf[:], -0.5))

            def inv_std(n):
                pool.wait_ge(mv_ready, n + 1)
                link(nc.gpsimd.tensor_scalar(veps[:, grp(n)], mv[:, grp(n), 1], EPS, None, ALU.add))
                nc.gpsimd.tensor_tensor(rstd[:, grp(n)], veps[:, grp(n)], mhalf[:], ALU.pow).then_inc(rstd_ready, 1)

            inv_std(0)
            inv_std(1)
            pool.wait_ge(w_in, 16)
            link(nc.gpsimd.tensor_copy(wj_hi[:], w[:, W_J:W_J + D]))
            nc.gpsimd.tensor_tensor(wj_lo[:], w[:, W_J:W_J + D], wj_hi[:].bitcast(F32), ALU.subtract).then_inc(wj_ready, 1)

            def mean_field(b):
                pool.wait_ge(sT_hi_ready, GB * (b + 1))
                link(nc.gpsimd.tensor_tensor(msum[:], ssum[:, 2 * b:2 * b + 1], ssum[:, 2 * b + 1:2 * b + 2], ALU.add))
                nc.gpsimd.tensor_scalar(meanb[:], c[:, C_ONE:C_ONE + P], msum[:, 0:1], 1.0 / N,
                                        ALU.mult, ALU.mult).then_inc(mean_ready, 1)

            def split_v(q):
                drained(pool, ("V", q))
                link(nc.gpsimd.tensor_copy(v_hi[:, grp(q), :], st[:, grp(q), :]))
                nc.gpsimd.tensor_tensor(v_lo[:, grp(q), :], st[:, grp(q), :], v_hi[:, grp(q), :].bitcast(F32),
                                        ALU.subtract).then_inc(v_ready, 1)

            def add_global(b):
                drained(pool, ("G", b))
                pool.wait_ge(v_ready, GB * (b + 1))
                rows = st[:, b * NT:(b + 1) * NT, :]
                nc.gpsimd.tensor_tensor(rows, rows, gb[:, b, :].unsqueeze(1).to_broadcast([P, NT, D]),
                                        ALU.add).then_inc(sg_ready, 1)

            def split_w13(e):
                pool.wait_ge(w13_in[e % 2], 16 * (e // 2 + 1))
                link(nc.gpsimd.tensor_copy(w13_hi[:, e, :], stage[:, e % 2, :]))
                nc.gpsimd.tensor_tensor(w13_lo[:, e, :], stage[:, e % 2, :], w13_hi[:, e, :].bitcast(F32),
                                        ALU.subtract).then_inc(w13_split, 1)

            def residual(g):
                pool.wait_ge(tanh_ready, g + 1)
                nc.gpsimd.tensor_tensor(xt[:, grp(g), :], xt[:, grp(g), :], arg[:, g % 2, :, :],
                                        ALU.add).then_inc(x1_ready, 1)

            def scatter(b):
                pool.wait_ge(slots_ready, b + 1)
                pool.wait_ge(xs_zeroed[b], 16)
                for t in range(NT):
                    for k in range(K):
                        nc.gpsimd.indirect_dma_start(
                            xs[b][:, :], bass.IndirectOffsetOnAxis(ap=slots[:, b, k, t:t + 1], axis=0),
                            xn[:, b * NT + t, :], None).then_inc(scattered[b], 16)

            def gather(b):
                for par in range(2):
                    pool.wait_ge(y_stored[par], 16 * (b + 1) * ST // QUAD)
                for t in range(NT):
                    if b > 0:
                        pool.wait_ge(out_ready, t + 1)
                    for k in range(K):
                        nc.gpsimd.indirect_dma_start(
                            st[:, k * NT + t, :], None, ys[b][:, :],
                            bass.IndirectOffsetOnAxis(ap=slots[:, b, k, t:t + 1], axis=0)).then_inc(gathered[t], 16)

            mean_field(0)
            split_v(0)
            split_v(1)
            add_global(0)
            inv_std(2)
            inv_std(3)
            mean_field(1)
            split_v(2)
            split_v(3)
            add_global(1)
            for g in range(GROUPS):
                if g < GROUPS - 1:
                    split_w13(3 * g)
                    if g < 2:
                        split_w13(3 * g + 1)
                        split_w13(3 * g + 2)
                    else:
                        split_w13(3 * g + 1)
                residual(g)
                inv_std(GROUPS + g)
                if g == 2:
                    scatter(0)
            scatter(1)
            gather(0)
            gather(1)

        @block.scalar
        def _(act):
            act.dma_start(c[:], cst).then_inc(c_in, 16)
            act.dma_start(w[:], wpack).then_inc(w_in, 16)
            act.wait_ge(c_in, 16)
            nc.scalar.copy(tri[:], c[:, C_TRI:C_TRI + P])
            nc.scalar.copy(ones[:], c[:, C_ONE:C_ONE + P]).then_inc(consts_ready, 1)

            def evac_xT(q):
                wait_misc(act, ("xT", q))
                nc.scalar.copy(xnT[:, cols(q)], misc(("xT", q))).then_inc(bank_free(("xT", q)), 1)

            def evac_sT_hi(q):
                wait_misc(act, ("sT", q))
                nc.scalar.activation(sT_hi[:, cols(q)], misc(("sT", q)), ACT.Identity, bias=w[:, B_COL:B_COL + 1],
                                     accum_out=ssum[:, q:q + 1]).then_inc(sT_hi_ready, 1)

            def evac_e_hi(g):
                wait_misc(act, ("e", g))
                nc.scalar.activation(e_hi[:, g % 2, :], misc(("e", g)), ACT.Copy, scale=SCALE).then_inc(e_hi_ready, 1)

            def evac_G(b):
                wait_misc(act, ("G", b))
                nc.scalar.copy(gb[:, b, :], misc(("G", b))[:, 0:D]).then_inc(bank_free(("G", b)), 1)

            def softmax_exp(i):
                act.wait_ge(max_ready, i + 1)
                nc.scalar.activation(probs[:, i % 2, :], S[:, i % 2, :], ACT.Exp, bias=nmax[:, i:i + 1],
                                     accum_out=L[:, i:i + 1]).then_inc(probs_ready, 1)

            def evac_pT_hi(i):
                g, r = divmod(i, GT)
                for k in range(2):
                    act.wait_ge(PT_full, 2 * i + k + 1)
                    nc.scalar.copy(pT_hi[:, g % 2, 4 * k:4 * k + 4, r * P:(r + 1) * P],
                                   PT[:, k, :].rearrange("p (c n) -> p c n", c=4)).then_inc(pT_hi_ready, 1)

            def evac_oT(g):
                wait_misc(act, ("AV", g))
                nc.scalar.copy(oT, misc(("AV", g))).then_inc(bank_free(("AV", g)), 1)

            def tanh(g):
                drained(act, ("OT", g))
                nc.scalar.activation(arg[:, g % 2, :, :], arg[:, g % 2, :, :], ACT.Tanh,
                                     scale=w[:, BETA:BETA + 1]).then_inc(tanh_ready, 1)

            def evac_x2T(g):
                wait_misc(act, ("X2", g))
                nc.scalar.copy(x2T, misc(("X2", g))).then_inc(bank_free(("X2", g)), 1)

            def gate_softmax_exp(b):
                act.wait_ge(gate_sub, b + 1)
                nc.scalar.activation(r64[:, 1, :, :], r64[:, 0, :, :], ACT.Exp).then_inc(gate_exp, 1)

            act.wait_ge(w_in, 16)
            evac_xT(0)
            evac_sT_hi(0)
            evac_xT(1)
            evac_sT_hi(1)
            evac_e_hi(0)
            evac_G(0)
            softmax_exp(0)
            softmax_exp(1)
            for i in range(TILES):
                g, r = divmod(i, GT)
                if r == 3 and g > 0:
                    evac_x2T(g - 1)
                evac_pT_hi(i)
                if i in (0, 1):
                    evac_xT(2 + i)
                    evac_sT_hi(2 + i)
                if i == 2:
                    evac_G(1)
                if r == 1 and g + 1 < GROUPS:
                    evac_e_hi(g + 1)
                if i + 2 < TILES:
                    softmax_exp(i + 2)
                if r == 0 and g > 0:
                    evac_oT(g - 1)
                if r == 1 and g > 0:
                    tanh(g - 1)
                if i == 11:
                    gate_softmax_exp(0)
            last = GROUPS - 1
            evac_oT(last)
            tanh(last)
            evac_x2T(last)
            gate_softmax_exp(1)

            def silu(t, u):
                act.wait_ge(gu_full, t + 1)
                nc.scalar.activation(sg[:, u, :], S[:, 0, u * 2 * H:u * 2 * H + H], ACT.Silu).then_inc(silu_ready, 1)

            def slotT_hi(t, u):
                act.wait_ge(slotT_full, t + 1)
                nc.scalar.copy(gT_hi[:, u, :], PT[:, 0, u * P:(u + 1) * P]).then_inc(slotT_hi_ready, 1)

            def evac_hT(t, u):
                act.wait_ge(hT_full, t + 1)
                nc.scalar.copy(hT[:, u, :], PT[:, 1, u * H:(u + 1) * H]).then_inc(hT_ready, 1)

            slotT_hi(0, 0)
            for t in range(QUAD):
                silu(t, t % 2)
                slotT_hi(t + 1, (t + 1) % 2)
                if t >= 1:
                    evac_hT(t - 1, (t - 1) % 2)
            with act.Fori(1, SLOT_TILES // QUAD - 1) as r:
                for v in range(QUAD):
                    silu(r * QUAD + v, v % 2)
                    slotT_hi(r * QUAD + v + 1, (v + 1) % 2)
                    evac_hT(r * QUAD + v - 1, (v + 1) % 2)
            for t in range(SLOT_TILES - QUAD, SLOT_TILES):
                silu(t, t % 2)
                if t + 1 < SLOT_TILES:
                    slotT_hi(t + 1, (t + 1) % 2)
                evac_hT(t - 1, (t - 1) % 2)
            evac_hT(SLOT_TILES - 1, (SLOT_TILES - 1) % 2)

        @block.vector
        def _(dve):
            steps = [0]

            def link(ins):
                steps[0] += 1
                ins.then_inc(dve_step, 1)
                dve.wait_ge(dve_step, steps[0])

            def stats(n):
                for j in range(GT):
                    ins = nc.vector.bn_stats(bn[:, n % 2, j, :], xt[:, (n % GROUPS) * GT + j, :])
                link(ins)
                for j in range(GT):
                    ins = nc.vector.bn_aggr(mv[:, n * GT + j, :], bn[:, n % 2, j, :])
                ins.then_inc(mv_ready, 1)

            def normalise(n):
                dve.wait_ge(rstd_ready, n + 1)
                if n >= GROUPS:
                    q = n - GROUPS
                for j in range(GT):
                    i = (n % GROUPS) * GT + j
                    ins = nc.vector.tensor_scalar(xn[:, i, :], xt[:, i, :], mv[:, n * GT + j, 0:1],
                                                  rstd[:, n * GT + j:n * GT + j + 1], ALU.subtract, ALU.mult)
                ins.then_inc(xn_ready, 1)

            def evac_sT_lo(q):
                dve.wait_ge(sT_hi_ready, q + 1)
                nc.vector.scalar_tensor_tensor(out=sT_lo[:, cols(q)], in0=misc(("sT", q)), scalar=w[:, B_COL:B_COL + 1],
                                               in1=sT_hi[:, cols(q)].bitcast(F32), op0=ALU.add,
                                               op1=ALU.subtract).then_inc(bank_free(("sT", q)), 1)

            def evac_e_lo(g):
                dve.wait_ge(e_hi_ready, g + 1)
                nc.vector.scalar_tensor_tensor(out=e_lo[:, g % 2, :], in0=misc(("e", g)), scalar=SCALE,
                                               in1=e_hi[:, g % 2, :].bitcast(F32), op0=ALU.mult,
                                               op1=ALU.subtract).then_inc(bank_free(("e", g)), 1)

            def evac_s(q):
                wait_misc(dve, ("V", q))
                ins = nc.vector.tensor_tensor(st[:, grp(q), :], misc(("V", q)).rearrange("p (t d) -> p t d", t=GT),
                                              w[:, B_ROW:B_ROW + D].unsqueeze(1).to_broadcast([P, GT, D]), ALU.add)
                ins.then_inc(bank_free(("V", q)), 1)

            def row_max(i):
                dve.wait_ge(S_full, i + 1)
                nc.vector.tensor_reduce(nmax[:, i:i + 1], S[:, i % 2, :], AXX, ALU.max, negate=True).then_inc(max_ready, 1)

            def evac_pT_lo(i):
                g, r = divmod(i, GT)
                for k in range(2):
                    dve.wait_ge(pT_hi_ready, 2 * i + k + 1)
                    part = (slice(None), g % 2, slice(4 * k, 4 * k + 4), slice(r * P, (r + 1) * P))
                    nc.vector.tensor_tensor(pT_lo[part], PT[:, k, :].rearrange("p (c n) -> p c n", c=4),
                                            pT_hi[part].bitcast(F32), ALU.subtract).then_inc(pT_ready, 1)

            def tanh_arg(g):
                link(nc.vector.reciprocal(rL[:, grp(g)], L[:, grp(g)]))
                wait_misc(dve, ("OT", g))
                dve.wait_ge(sg_ready, g // GB + 1)
                for j in range(GT):
                    i = g * GT + j
                    ins = nc.vector.scalar_tensor_tensor(out=arg[:, g % 2, j, :], in0=misc(("OT", g))[:, j * P:(j + 1) * P],
                                                         scalar=rL[:, i:i + 1], in1=st[:, i, :], op0=ALU.mult, op1=ALU.add)
                ins.then_inc(bank_free(("OT", g)), 1)

            def stats_after(g):
                dve.wait_ge(x1_ready, g + 1)
                stats(GROUPS + g)

            def take_logits(g):
                wait_misc(dve, ("LG", g))
                nc.vector.tensor_copy(lg[:, grp(g), :], misc(("LG", g))[:, 0:GT * E].rearrange("p (t e) -> p t e", e=E)
                                      ).then_inc(bank_free(("LG", g)), 1)

            def col(n):
                return r8[:, n, :]

            def bc(ap):
                return ap.unsqueeze(2).to_broadcast([P, NT, E])

            def gate_max(b):
                drained(dve, ("LG", GB * b + 1))
                rows = lg[:, b * NT:(b + 1) * NT, :]
                link(nc.vector.tensor_reduce(col(0), rows, AXX, ALU.max))
                nc.vector.tensor_tensor(r64[:, 0, :, :], rows, bc(col(0)), ALU.subtract).then_inc(gate_sub, 1)

            def choose(b):
                dve.wait_ge(gate_exp, b + 1)
                ex = r64[:, 1, :, :]
                desc = c[:, C_DESC:C_DESC + E].unsqueeze(1).to_broadcast([P, NT, E])
                link(nc.vector.tensor_reduce(col(1), ex, AXX, ALU.add))
                link(nc.vector.reciprocal(col(2), col(1)))
                link(nc.vector.tensor_tensor(scores[:], ex, bc(col(2)), ALU.mult))
                for k in range(K):
                    best = gate[:, b * NT:(b + 1) * NT, k]
                    link(nc.vector.tensor_reduce(best, scores[:], AXX, ALU.max))
                    link(nc.vector.tensor_tensor(r64[:, 2, :, :], scores[:], bc(best), ALU.is_equal))
                    link(nc.vector.tensor_tensor(r64[:, 3, :, :], r64[:, 2, :, :], desc, ALU.mult))
                    link(nc.vector.tensor_reduce(col(3), r64[:, 3, :, :], AXX, ALU.max))
                    link(nc.vector.tensor_tensor(hot[:, k, :, :], r64[:, 3, :, :], bc(col(3)), ALU.is_equal))
                    if k == 0:
                        link(nc.vector.scalar_tensor_tensor(out=scores[:], in0=hot[:, 0, :, :], scalar=-2.0,
                                                            in1=scores[:], op0=ALU.mult, op1=ALU.add))
                nc.vector.tensor_tensor(sel[:], hot[:, 0, :, :], hot[:, 1, :, :], ALU.add).then_inc(sel_ready, 1)

            def place(b):
                wait_misc(dve, ("R", b))
                rank = misc(("R", b))[:, 0:NT * E].rearrange("p (t e) -> p t e", e=E)
                count = misc(("R", b))[:, NT * E:NT * E + E]
                thr = c[:, C_THR:C_THR + N // P].unsqueeze(1).to_broadcast([P, E, N // P])
                link(nc.vector.tensor_tensor(cmp[:], count.unsqueeze(2).to_broadcast([P, E, N // P]), thr, ALU.is_gt))
                link(nc.vector.tensor_reduce(tiles_e[:], cmp[:], AXX, ALU.add))
                link(nc.vector.tensor_tensor(cmp[:], tiles_e[:].unsqueeze(1).to_broadcast([P, E, E]),
                                             c[:, C_LT:C_LT + E * E].rearrange("p (e f) -> p e f", f=E), ALU.mult))
                link(nc.vector.tensor_reduce(base[:], cmp[:], AXX, ALU.add))
                link(nc.vector.tensor_tensor(ends[:], base[:], tiles_e[:], ALU.add))
                link(nc.vector.tensor_tensor(cmpj[:], ends[0:1, :].unsqueeze(1).to_broadcast([1, ST, E]),
                                             c[0:1, C_J:C_J + ST].unsqueeze(2).to_broadcast([1, ST, E]), ALU.is_le))
                link(nc.vector.tensor_reduce(tabf[:], cmpj[:], AXX, ALU.add))
                link(nc.vector.tensor_scalar(tab[:, b * ST:(b + 1) * ST], tabf[:], float(E - 1), None, ALU.min))
                nc.vector.scalar_tensor_tensor(out=r64[:, 4, :, :], in0=base[:].unsqueeze(1).to_broadcast([P, NT, E]),
                                               scalar=float(P), in1=rank, op0=ALU.mult,
                                               op1=ALU.add).then_inc(bank_free(("R", b)), 1)
                drained(dve, ("R", b))
                for k in range(K):
                    link(nc.vector.tensor_tensor(r64[:, 5, :, :], hot[:, k, :, :], r64[:, 4, :, :], ALU.mult))
                    link(nc.vector.tensor_reduce(slotf[:, k, :], r64[:, 5, :, :], AXX, ALU.add))
                ins = nc.vector.tensor_scalar(slots[:, b, :, :], slotf[:], float(ST * P - 1), None, ALU.min)
                ins.then_inc(slots_ready, 1)

            def combine(b):
                for t in range(NT):
                    i = b * NT + t
                    dve.wait_ge(gathered[t], 16 * K * (b + 1))
                    for k in range(K):
                        ins = nc.vector.scalar_tensor_tensor(out=xt[:, i, :], in0=st[:, k * NT + t, :],
                                                             scalar=gate[:, i, k:k + 1], in1=xt[:, i, :],
                                                             op0=ALU.mult, op1=ALU.add)
                        if k == 0:
                            link(ins)
                    ins.then_inc(out_ready, 1)

            for q in range(2):
                dve.wait_ge(x_in[q], 16)
                stats(q)
            normalise(0)
            normalise(1)
            dve.wait_ge(w_in, 16)
            evac_sT_lo(0)
            evac_sT_lo(1)
            evac_e_lo(0)
            evac_s(0)
            evac_s(1)
            row_max(0)
            row_max(1)
            dve.wait_ge(x_in[2], 16)
            stats(2)
            stats(3)
            normalise(2)
            normalise(3)
            for i in range(TILES):
                g, r = divmod(i, GT)
                if r == 3 and g > 0:
                    normalise(GROUPS + g - 1)
                evac_pT_lo(i)
                if i in (0, 1):
                    evac_sT_lo(2 + i)
                if i == 2:
                    evac_s(2)
                    evac_s(3)
                if r == 1 and g + 1 < GROUPS:
                    evac_e_lo(g + 1)
                if i == 12:
                    choose(0)
                if i + 2 < TILES:
                    row_max(i + 2)
                if r == 1 and g > 0:
                    tanh_arg(g - 1)
                if r == 2 and g > 0:
                    stats_after(g - 1)
                if r == 3 and g > 0:
                    take_logits(g - 1)
                if i == 11:
                    gate_max(0)
                if i == 12:
                    place(0)
            last = GROUPS - 1
            tanh_arg(last)
            stats_after(last)
            normalise(GROUPS + last)
            take_logits(last)
            gate_max(1)
            choose(1)
            place(1)

            def hidden(t, u):
                dve.wait_ge(silu_ready, t + 1)
                nc.vector.tensor_tensor(h[:, u, :], sg[:, u, :], S[:, 0, u * 2 * H + H:(u + 1) * 2 * H],
                                        ALU.mult).then_inc(h_ready, 1)

            def slotT_lo(t, u):
                dve.wait_ge(slotT_hi_ready, t + 1)
                nc.vector.tensor_tensor(gT_lo[:, u, :], PT[:, 0, u * P:(u + 1) * P], gT_hi[:, u, :].bitcast(F32),
                                        ALU.subtract).then_inc(slotT_ready, 1)

            def evac_y(t, v, stored):
                dve.wait_ge(y_full, t + 1)
                if stored is not None and v % 2 == 0:
                    dve.wait_ge(y_stored[v // 2], 16 * stored)
                nc.vector.tensor_copy(y[:, v, :], S[:, 1, (v % 2) * GW:(v % 2) * GW + D]).then_inc(y_ready, 1)

            slotT_lo(0, 0)
            for t in range(QUAD):
                hidden(t, t % 2)
                slotT_lo(t + 1, (t + 1) % 2)
                if t >= 2:
                    evac_y(t - 2, t - 2, None)

            def quads(lo, hi):
                with dve.Fori(lo, hi) as r:
                    for v in range(QUAD):
                        hidden(r * QUAD + v, v % 2)
                        slotT_lo(r * QUAD + v + 1, (v + 1) % 2)
                        if v < 2:
                            evac_y(r * QUAD + v - 2, v + 2, r - 1 if lo > 1 else None)
                        else:
                            evac_y(r * QUAD + v - 2, v - 2, r)

            def first_quad():
                for t in range(QUAD, 2 * QUAD):
                    hidden(t, t % 2)
                    slotT_lo(t + 1, (t + 1) % 2)
                    evac_y(t - 2, (t - 2) % 4, 1 if t >= QUAD + 2 else None)

            first_quad()
            mid = ST // QUAD + 3
            quads(2, mid)
            combine(0)
            quads(mid, SLOT_TILES // QUAD - 1)
            for t in range(SLOT_TILES - QUAD, SLOT_TILES):
                hidden(t, t % 2)
                if t + 1 < SLOT_TILES:
                    slotT_lo(t + 1, (t + 1) % 2)
                evac_y(t - 2, (t - 2) % 4, (t - 2) // 4)
            for t in range(SLOT_TILES - 2, SLOT_TILES):
                evac_y(t, t % 4, t // 4)
            combine(1)

        @block.tensor
        def _(pe):
            def take(use):
                n = MISC[use]
                if n >= 2:
                    pe.wait_ge(misc_free[n % 2], n // 2)

            def matmul3(dst, w_hi, w_lo, m_hi, m_lo, start, stop):
                pe.matmul(dst, w_hi, m_hi, start=start, stop=False)
                pe.matmul(dst, w_hi, m_lo, start=False, stop=False)
                return pe.matmul(dst, w_lo, m_hi, start=False, stop=stop)

            def transposes(use, src):
                take(use)
                for j in range(GT):
                    ins = pe.transpose(misc(use)[:, j * P:(j + 1) * P], src(j), ident)
                ins.then_inc(misc_full, 1)

            def xT(q):
                pe.wait_ge(xn_ready, q + 1)
                transposes(("xT", q), lambda j: xn[:, q * GT + j, :])

            def sT(q):
                take(("sT", q))
                drained(pe, ("xT", q))
                pe.matmul(misc(("sT", q)), w[:, W_SPIN:W_SPIN + D], xnT[:, cols(q)], start=True,
                          stop=True).then_inc(misc_full, 1)

            def V(q):
                take(("V", q))
                for j in range(GT):
                    i = q * GT + j
                    ins = pe.matmul(misc(("V", q))[:, j * P:(j + 1) * P], xnT[:, i * P:(i + 1) * P],
                                    w[:, W_SPIN:W_SPIN + D], start=True, stop=True)
                ins.then_inc(misc_full, 1)

            def G(b):
                take(("G", b))
                pe.wait_ge(mean_ready, b + 1)
                pe.matmul(misc(("G", b))[:, 0:D], meanb[:], w[:, W_GLOB:W_GLOB + D], start=True,
                          stop=True).then_inc(misc_full, 1)

            def energies(g):
                take(("e", g))
                if g == 0:
                    pe.wait_ge(wj_ready, 1)
                drained(pe, ("sT", g))
                matmul3(misc(("e", g)), wj_hi[:], wj_lo[:], sT_hi[:, cols(g)], sT_lo[:, cols(g)], True,
                        True).then_inc(misc_full, 1)

            def scores_of(i):
                g, r = divmod(i, GT)
                b = i // NT
                if r == 0:
                    drained(pe, ("e", g))
                q = slice(r * P, (r + 1) * P)
                for k in range(GB):
                    ins = matmul3(S[:, i % 2, k * GW:(k + 1) * GW], e_hi[:, g % 2, q], e_lo[:, g % 2, q],
                                  sT_hi[:, cols(GB * b + k)], sT_lo[:, cols(GB * b + k)], True, True)
                ins.then_inc(S_full, 1)

            def transpose_probs(i):
                pe.wait_ge(probs_ready, i + 1)
                for k in range(2):
                    if i > 0:
                        pe.wait_ge(pT_ready, 2 * (i - 1) + k + 1)
                    for m in range(4):
                        ch = 4 * k + m
                        ins = pe.transpose(PT[:, k, m * P:(m + 1) * P], probs[:, i % 2, ch * P:(ch + 1) * P], ident)
                    ins.then_inc(PT_full, 1)

            def AV(g):
                take(("AV", g))
                b = g // GB
                pe.wait_ge(v_ready, GB * (b + 1))
                pe.wait_ge(pT_ready, 2 * GT * (g + 1))
                for ch in range(CH):
                    i = b * NT + ch
                    ins = matmul3(misc(("AV", g)), v_hi[:, i, :], v_lo[:, i, :], pT_hi[:, g % 2, ch, :],
                                  pT_lo[:, g % 2, ch, :], ch == 0, ch == CH - 1)
                ins.then_inc(misc_full, 1)

            def OT(g):
                drained(pe, ("AV", g))
                transposes(("OT", g), lambda j: oT[:, j * P:(j + 1) * P])

            def X2(g):
                pe.wait_ge(xn_ready, GROUPS + g + 1)
                transposes(("X2", g), lambda j: xn[:, g * GT + j, :])

            def LG(g):
                take(("LG", g))
                drained(pe, ("X2", g))
                for j in range(GT):
                    ins = pe.matmul(misc(("LG", g))[:, j * E:(j + 1) * E], x2T[:, j * P:(j + 1) * P],
                                    w[:, W_GATE:W_GATE + E], start=True, stop=True)
                ins.then_inc(misc_full, 1)

            def R(b):
                take(("R", b))
                pe.wait_ge(sel_ready, b + 1)
                bank = misc(("R", b))
                rank = bank[:, 0:NT * E].rearrange("p (t e) -> p t e", e=E)
                pe.matmul(rank, tri[:], sel[:], start=True, stop=True, skip_group_check=True)
                for t in range(NT - 1):
                    pe.matmul(rank[:, t + 1:NT, :], ones[:], sel[:, t:t + 1, :].to_broadcast([P, NT - 1 - t, E]),
                              start=False, stop=True, skip_group_check=True)
                for t in range(NT):
                    ins = pe.matmul(bank[:, NT * E:NT * E + E], ones[:], sel[:, t, :], start=(t == 0),
                                    stop=(t == NT - 1))
                ins.then_inc(misc_full, 1)

            pe.wait_ge(c_in, 16)
            pe.wait_ge(w_in, 16)
            xT(0)
            sT(0)
            xT(1)
            sT(1)
            energies(0)
            V(0)
            V(1)
            G(0)
            scores_of(0)
            scores_of(1)
            for i in range(TILES):
                g, r = divmod(i, GT)
                if r == 3 and g > 0:
                    X2(g - 1)
                transpose_probs(i)
                if i in (0, 1):
                    xT(2 + i)
                    sT(2 + i)
                if i == 2:
                    V(2)
                    V(3)
                    G(1)
                if r == 1 and g + 1 < GROUPS:
                    energies(g + 1)
                if i + 2 < TILES:
                    scores_of(i + 2)
                if r == 0 and g > 0:
                    AV(g - 1)
                if i == 12:
                    pe.wait_ge(consts_ready, 1)
                    R(0)
                if r == 1 and g > 0:
                    OT(g - 1)
                if r == 3 and g > 0:
                    LG(g - 1)
            last = GROUPS - 1
            AV(last)
            OT(last)
            X2(last)
            LG(last)
            R(1)

            def slotT(t, u, v, loads):
                if v % 2 == 0:
                    pe.wait_ge(slot_loaded[v // 2], 16 * loads)
                pe.transpose(PT[:, 0, u * P:(u + 1) * P], xs_in[:, v, :], ident).then_inc(slotT_full, 1)

            def gate_up(t, u, h_of):
                e = pe.value_load(tab[0:1, bass.ds(t, 1)], min_val=0, max_val=E - 1)
                pe.wait_ge(slotT_ready, t + 1)
                if h_of is not None:
                    pe.wait_ge(h_ready, h_of)
                bank = S[:, 0, u * 2 * H:(u + 1) * 2 * H]
                hi, lo = w13_hi[:, bass.ds(e, 1), :].rearrange("p a n -> p (a n)"), w13_lo[:, bass.ds(e, 1), :].rearrange("p a n -> p (a n)")
                pe.matmul(bank, gT_hi[:, u, :], hi, start=True, stop=False)
                pe.matmul(bank, gT_hi[:, u, :], lo, start=False, stop=False)
                pe.matmul(bank, gT_lo[:, u, :], hi, start=False, stop=True).then_inc(gu_full, 1)

            def hiddenT(t, u):
                pe.wait_ge(h_ready, t + 1)
                for k in range(2):
                    ins = pe.transpose(PT[:, 1, u * H + k * P:u * H + (k + 1) * P], h[:, u, k * P:(k + 1) * P], ident)
                ins.then_inc(hT_full, 1)

            def down(t, u, y_of):
                e = pe.value_load(tab[0:1, bass.ds(t, 1)], min_val=0, max_val=E - 1)
                pe.wait_ge(hT_ready, t + 1)
                if y_of is not None:
                    pe.wait_ge(y_ready, y_of)
                for k in range(2):
                    ins = pe.matmul(S[:, 1, u * GW:u * GW + D], hT[:, u, k * P:(k + 1) * P],
                                    w2s[:, bass.ds(e, 1), k, :].rearrange("p a n -> p (a n)"), start=(k == 0), stop=(k == 1))
                ins.then_inc(y_full, 1)

            pe.wait_ge(w13_split, E)
            pe.wait_ge(w2_in, 16)
            slotT(0, 0, 0, 1)
            for t in range(QUAD):
                gate_up(t, t % 2, t - 1 if t >= 2 else None)
                slotT(t + 1, (t + 1) % 2, (t + 1) % 4, (t + 1) // 4 + 1)
                if t >= 2:
                    down(t - 2, t % 2, None)
                if t >= 1:
                    hiddenT(t - 1, (t - 1) % 2)
            with pe.Fori(1, SLOT_TILES // QUAD - 1) as r:
                for v in range(QUAD):
                    t = r * QUAD + v
                    gate_up(t, v % 2, t - 1)
                    slotT(t + 1, (v + 1) % 2, (v + 1) % 4, r + 1 + (v + 1) // 4)
                    down(t - 2, v % 2, t - 3)
                    hiddenT(t - 1, (v + 1) % 2)
            for t in range(SLOT_TILES - QUAD, SLOT_TILES):
                gate_up(t, t % 2, t - 1)
                if t + 1 < SLOT_TILES:
                    slotT(t + 1, (t + 1) % 2, (t + 1) % 4, (t + 1) // 4 + 1)
                down(t - 2, t % 2, t - 3)
                hiddenT(t - 1, (t - 1) % 2)
            down(SLOT_TILES - 2, 0, SLOT_TILES - 3)
            hiddenT(SLOT_TILES - 1, 1)
            down(SLOT_TILES - 1, 1, SLOT_TILES - 2)


def kernel(L0_attn_x, L0_attn_W_spin, L0_attn_b_spin, L0_attn_W_global, L0_attn_W_J, L0_attn_beta,
           L0_ffn_gate_w, L0_ffn_w1, L0_ffn_w2, L0_ffn_w3):
    import concourse.bacc as bacc
    from concourse.bass_utils import run_bass_kernel_spmd

    b = np.asarray(L0_attn_b_spin)
    wpack = np.concatenate([
        np.asarray(L0_attn_W_spin).T, np.asarray(L0_attn_W_J).T, np.asarray(L0_attn_W_global).T,
        np.broadcast_to(b[None, :], (P, D)), np.asarray(L0_ffn_gate_w).T, b[:, None],
        np.broadcast_to(np.asarray(L0_attn_beta)[None, :], (P, 1))], axis=1)
    w13 = np.concatenate([np.asarray(L0_ffn_w1), np.asarray(L0_ffn_w3)], axis=2).transpose(1, 0, 2)
    w2 = np.asarray(L0_ffn_w2).reshape(E, 2, P, D).transpose(2, 0, 1, 3)
    arrays = {"x": np.asarray(L0_attn_x), "wpack": wpack, "cst": constants(), "w13": w13, "w2": w2}
    arrays = {k: np.ascontiguousarray(v) for k, v in arrays.items()}

    nc = bacc.Bacc("TRN2", target_bir_lowering=False, num_devices=1)
    ins = [nc.dram_tensor(k, v.shape, F32, kind="ExternalInput").ap() for k, v in arrays.items()]
    xs = [nc.dram_tensor(f"xs{i}", (ST * P, D), F32).ap() for i in range(NB)]
    ys = [nc.dram_tensor(f"ys{i}", (ST * P, D), F32).ap() for i in range(NB)]
    out = nc.dram_tensor("out", (NB, N, D), F32, kind="ExternalOutput").ap()
    build(nc, *ins, xs, ys, out)
    r = run_bass_kernel_spmd(nc, [arrays], core_ids=[0])
    return r.results[0]["out"]
```

```python
from contextlib import ExitStack

import numpy as np

import concourse.bass as bass
from concourse import mybir

ALU = mybir.AluOpType
ACT = mybir.ActivationFunctionType
AXX = mybir.AxisListType.X
F32 = mybir.dt.float32
F32R = mybir.dt.float32r
BF16 = mybir.dt.bfloat16
U32 = mybir.dt.uint32
I32 = mybir.dt.int32

P = 128
D = 128
E = 8
H = 256
K = 2
NB = 2
N = 1024
NT = N // P
TILES = NB * NT
GT = 4
GW = GT * P
GROUPS = TILES // GT
GB = NT // GT
CH = N // P
EPS = 1e-5
SCALE = float(D) ** -0.5
QUAD = 4
ROUND = 2 * QUAD
PLACES = 4
LAG = 5
ST = -(-(K * N // P + E - 1) // QUAD) * QUAD
SLOT_TILES = NB * ST
PAIRS = ST // 2

W_SPIN, W_J, W_GLOB, B_ROW, W_GATE, B_COL, BETA, W_COLS = 0, 128, 256, 384, 512, 520, 521, 522
C_ID, C_TRI, C_DESC, C_THR, C_LT, C_J, C_COLS = 0, 128, 256, 264, 272, 336, 336 + ST


def constants():
    c = np.zeros((P, C_COLS), np.float32)
    c[:, C_ID:C_ID + P] = np.eye(P)
    c[:, C_TRI:C_TRI + P] = np.triu(np.ones((P, P)), 1)
    c[:, C_DESC:C_DESC + E] = np.arange(E, 0, -1)
    c[:, C_THR:C_THR + N // P] = np.arange(N // P) * P
    c[:, C_LT:C_LT + E * E] = np.tril(np.ones((E, E)), -1).reshape(-1)
    c[:, C_J:C_J + ST] = np.arange(ST)
    return c


START = [("xT", 0), ("xT", 1), ("sT", 0), ("sT", 1), ("e", 0), ("V", 0), ("V", 1), ("G", 0)]
BEFORE = {1: [("e", 1)], 2: [("xT", 2)], 3: [("xT", 3)], 4: [("V", 2)], 5: [("e", 2), ("V", 3)], 6: [("G", 1)],
          7: [("e", 3)], 8: [("OT", 0)], 9: [("OT", 1)], 10: [("X2", 0)], 11: [("X2", 1)], 12: [("R", 0)]}
AFTER = {2: [("sT", 2)], 3: [("sT", 3)], 4: [("AV", 0)], 5: [("AV", 0)], 6: [("AV", 0)], 7: [("AV", 0)],
         8: [("AV", 1)], 10: [("LG", 0)], 11: [("LG", 1)], 12: [("AV", 2)], 13: [("AV", 2)],
         14: [("AV", 2)], 15: [("AV", 2), ("AV", 3), ("OT", 2), ("AV", 3)]}
LATE = {0: [("X2", 2)], 1: [("LG", 2)], 3: [("X2", 3)], 4: [("LG", 3)], 6: [("R", 1)]}
ORDER = (START + [use for i in range(TILES) for use in BEFORE.get(i, []) + AFTER.get(i, [])] + [("OT", 3)] +
         [use for t in sorted(LATE) for use in LATE[t]])


def banks():
    first, last = ORDER.index(("AV", 0)), max(n for n, use in enumerate(ORDER) if use == ("AV", 2))
    place, turns = {}, [0, 0]
    for n, use in enumerate(ORDER):
        if use not in place:
            k = int(use[0] == "AV") if first <= n <= last else len(place) % 2
            place[use] = (k, turns[k])
            turns[k] += 1
    return place


MISC = banks()


def build(nc, x, wpack, cst, w13, w2, xs, ys, out):
    ctx = ExitStack()
    with ctx:
        def sb(name, shape, dt=F32):
            return ctx.enter_context(nc.sbuf_tensor(name, shape, dt))

        def sem(name):
            return ctx.enter_context(nc.semaphore(name))

        xt = sb("x_tokens", [P, TILES, D])
        xn = sb("x_normed", [P, TILES, D])
        xnT = sb("x_normed_T", [P, TILES * P])
        sT_hi = sb("sT_hi", [P, TILES * P], F32R)
        sT_lo = sb("sT_lo", [P, TILES * P], F32R)
        e_hi = sb("e_hi", [P, 2, GW], F32R)
        e_lo = sb("e_lo", [P, 2, GW], F32R)
        st = sb("s_tokens", [P, TILES, D])
        v_hi = sb("v_hi", [P, TILES, D], F32R)
        v_lo = sb("v_lo", [P, TILES, D], F32R)
        probs = sb("probs", [P, 2, N])
        pT_hi = sb("pT_hi", [P, 2, CH, GW], F32R)
        pT_lo = sb("pT_lo", [P, 2, CH, GW], F32R)
        arg = sb("tanh_arg", [P, 2, GT, D])
        w = sb("w_packed", [P, W_COLS])
        c = sb("constants", [P, C_COLS])
        tri = sb("tri_bf", [P, P], BF16)
        ones = sb("ones_bf", [P, P], BF16)
        wj_hi = sb("wj_hi", [P, D], F32R)
        wj_lo = sb("wj_lo", [P, D], F32R)
        stage = sb("w13_stage", [P, 4, 2 * H])
        w13_hi = sb("w13_hi", [P, E, 2 * H], F32R)
        w13_lo = sb("w13_lo", [P, E, 2 * H], F32R)
        w2s = sb("w2_rows", [P, E, 2, D])
        zero = sb("zero", [P, D])
        bn = sb("bn_stats", [P, 2, GT, 6])
        mv = sb("mean_var", [P, 2 * TILES, 2])
        rstd = sb("rstd", [P, 2 * TILES])
        veps = sb("var_eps", [P, 2 * TILES])
        mhalf = sb("minus_half", [P, GT])
        ssum = sb("s_sums", [P, GROUPS])
        msum = sb("s_sum", [P, 1])
        meanb = sb("mean_bcast", [P, P])
        gb = sb("global_influence", [P, NB, D])
        nmax = sb("neg_max", [P, TILES])
        L = sb("exp_sums", [P, TILES])
        rL = sb("exp_sums_inv", [P, TILES])
        lg = sb("logits", [P, TILES, E])
        r8 = sb("route_cols", [P, 6, NT])
        r64 = sb("route_rows", [P, 6, NT, E])
        hot = sb("chosen", [P, K, NT, E])
        sel = sb("selected_bf", [P, NT, E], BF16)
        gate = sb("gate_values", [P, NB, K, NT])
        cmp = sb("compare", [P, E, E])
        tiles_e = sb("tiles_of_expert", [P, E])
        base = sb("first_tile", [P, E])
        ends = sb("end_tile", [P, E])
        slotf = sb("slots_f", [P, K, NT])
        slots = sb("slots", [P, NB, K, NT], U32)
        tabf = sb("tile_expert_f", [1, ST])
        tab = sb("tile_expert", [1, SLOT_TILES], I32)

        oT = xnT[:, 0:GW]
        x2T = xnT[:, GW:2 * GW]
        xs_in = pT_lo[:, 0, 0:2, :].bitcast(F32).rearrange("p c (v d) -> p (c v) d", d=D)
        cmpj = gb[0:1, :, :].rearrange("p b d -> p (b d)")[:, 0:ST * E].rearrange("p (j e) -> p j e", e=E)
        prod = meanb[:].rearrange("p (k t e) -> p k t e", k=K, e=E)
        sg = xnT[:, 2 * GW:2 * GW + 2 * H].rearrange("p (u n) -> p u n", u=2)
        h = xnT[:, 3 * GW:3 * GW + 2 * H].rearrange("p (u n) -> p u n", u=2)
        gT_hi = e_hi[:, :, 0:P]
        gT_lo = e_lo[:, :, 0:P]
        hT = probs[:, 0, 0:2 * H].rearrange("p (u n) -> p u n", u=2)
        y = probs[:, 1, 0:4 * D].rearrange("p (v n) -> p v n", v=4)

        rows_of = [st, xn]

        ident = c[:, C_ID:C_ID + P]

        S = ctx.enter_context(nc.psum_tensor("S", [P, 2, N], F32))
        PT = ctx.enter_context(nc.psum_tensor("PT", [P, 2, GW], F32))
        MI = ctx.enter_context(nc.psum_tensor("MI", [P, 2, GW], F32))

        x_in = [sem(f"x_in{q}") for q in range(3)]
        w_in = sem("w_in")
        c_in = sem("c_in")
        w2_in = sem("w2_in")
        w13_in = [sem(f"w13_in{k}") for k in range(4)]
        w13_split = sem("w13_split")
        consts_ready = sem("consts_ready")
        wj_ready = sem("wj_ready")
        zero_ready = sem("zero_ready")
        xs_zeroed = [sem(f"xs_zeroed{b}") for b in range(NB)]
        mv_ready = sem("mv_ready")
        rstd_ready = sem("rstd_ready")
        xn_ready = sem("xn_ready")
        misc_full = [sem(f"misc_full{k}") for k in range(2)]
        misc_free = [sem(f"misc_free{k}") for k in range(2)]
        sT_hi_ready = sem("sT_hi_ready")
        e_hi_ready = sem("e_hi_ready")
        mean_ready = sem("mean_ready")
        v_ready = sem("v_ready")
        sg_ready = sem("sG_ready")
        S_full = sem("S_full")
        max_ready = sem("max_ready")
        probs_ready = sem("probs_ready")
        PT_full = sem("PT_full")
        pT_hi_ready = sem("pT_hi_ready")
        pT_ready = sem("pT_ready")
        tanh_ready = sem("tanh_ready")
        x1_ready = sem("x1_ready")
        gate_sub = sem("gate_sub")
        gate_exp = sem("gate_exp")
        sel_ready = sem("sel_ready")
        slots_ready = sem("slots_ready")
        scattered = [sem(f"scattered{b}") for b in range(NB)]
        dve_step = sem("dve_step")
        pool_step = sem("pool_step")
        slot_loaded = [sem(f"slot_loaded{k}") for k in range(PLACES)]
        slotT_full = sem("slotT_full")
        slotT_hi_ready = sem("slotT_hi_ready")
        slotT_ready = sem("slotT_ready")
        gu_full = sem("gu_full")
        silu_ready = sem("silu_ready")
        h_ready = sem("h_ready")
        hT_full = sem("hT_full")
        hT_ready = sem("hT_ready")
        y_full = sem("y_full")
        y_ready = sem("y_ready")
        y_stored = [sem(f"y_stored{k}") for k in range(2)]
        gathered = [[sem(f"gathered{b}_{t}") for t in range(NT)] for b in range(NB)]
        out_ready = sem("out_ready")
        out_done = sem("out_done")

        def grp(g):
            return slice(g * GT, (g + 1) * GT)

        def cols(g):
            return slice(g * GW, (g + 1) * GW)

        def misc(use):
            return MI[:, MISC[use][0], :]

        def bank_free(use):
            return misc_free[MISC[use][0]]

        def drained(eng, use):
            eng.wait_ge(bank_free(use), MISC[use][1] + 1)

        def wait_misc(eng, use):
            eng.wait_ge(misc_full[MISC[use][0]], MISC[use][1] + 1)

        xg = [x[0, :, :].rearrange("(p t) d -> p t d", t=NT)[:, 0:GT, :],
              x[0, :, :].rearrange("(p t) d -> p t d", t=NT)[:, GT:NT, :],
              x[1, :, :].rearrange("(p t) d -> p t d", t=NT)]
        out_v = out.rearrange("b (p t) d -> p b t d", t=NT)
        xs_pairs = [a.rearrange("(n u p) d -> n p u d", u=2, p=P) for a in xs]
        ys_pairs = [a.rearrange("(n u p) d -> n p u d", u=2, p=P) for a in ys]

        block = ctx.enter_context(nc.Block())

        @block.sync
        def _(sp):
            sp.dma_start(xt[:, 0:GT, :], xg[0]).then_inc(x_in[0], 16)
            sp.dma_start(xt[:, GT:NT, :], xg[1]).then_inc(x_in[1], 16)
            sp.dma_start(xt[:, NT:TILES, :], xg[2]).then_inc(x_in[2], 16)
            for e in range(E):
                if e >= 4:
                    sp.wait_ge(w13_split, e - 3)
                sp.dma_start(stage[:, e % 4, :], w13[:, e, :]).then_inc(w13_in[e % 4], 16)
                if e == 3:
                    sp.dma_start(w2s[:], w2).then_inc(w2_in, 16)
                    sp.wait_ge(zero_ready, 1)
                    for b in range(NB):
                        sp.dma_start(xs[b].rearrange("(n p) d -> p n d", p=P),
                                     zero[:].unsqueeze(1).to_broadcast([P, ST, D])).then_inc(xs_zeroed[b], 16)

            def load_pair(n, b, k, place, free=None):
                if free is not None:
                    sp.wait_ge(slotT_full, free)
                sp.dma_start(xs_in[:, 2 * place:2 * place + 2, :], xs_pairs[b][k]).then_inc(slot_loaded[place], 16)

            def store_pair(n, b, k, par):
                sp.wait_ge(y_ready, 2 * n + 2)
                sp.dma_start(ys_pairs[b][k], y[:, 2 * par:2 * par + 2, :]).then_inc(y_stored[par], 16)

            drained(sp, ("AV", 2))
            for b in range(NB):
                sp.wait_ge(scattered[b], 16 * K * NT)
                first = PLACES if b == 0 else LAG
                first += (PAIRS - first) % PLACES
                for k in range(first):
                    n = b * PAIRS + k
                    load_pair(n, b, k, n % PLACES, 2 * (n - PLACES) + 2 if n >= PLACES else None)
                    if n >= LAG:
                        store_pair(n - LAG, (n - LAG) // PAIRS, (n - LAG) % PAIRS, (n - LAG) % 2)
                if b == 0:
                    for k in range(first, first + PLACES):
                        load_pair(k, b, k, k % PLACES, 2 * (k - PLACES) + 2)
                        if k >= LAG:
                            store_pair(k - LAG, b, k - LAG, (k - LAG) % 2)
                    first += PLACES
                n0 = b * PAIRS + first
                with sp.Fori(0, (PAIRS - first) // PLACES) as r:
                    for u in range(PLACES):
                        k = PLACES * r + first + u
                        n = PLACES * r + n0 + u
                        load_pair(n, b, k, (n0 + u) % PLACES, 2 * PLACES * r + 2 * (n0 + u - PLACES) + 2)
                        store_pair(n - LAG, b, k - LAG, (n0 + u - LAG) % 2)
            for n in range(SLOT_TILES // 2 - LAG, SLOT_TILES // 2):
                store_pair(n, n // PAIRS, n % PAIRS, n % 2)
            for b in range(NB):
                for t in range(0, NT, 2):
                    sp.wait_ge(out_ready, b * NT + t + 2)
                    sp.dma_start(out_v[:, b, t:t + 2, :], xt[:, b * NT + t:b * NT + t + 2, :]).then_inc(out_done, 16)
            sp.wait_ge(out_done, 16 * NB * NT // 2)

        @block.gpsimd
        def _(pool):
            steps = [0]

            def link(ins):
                steps[0] += 1
                ins.then_inc(pool_step, 1)
                pool.wait_ge(pool_step, steps[0])

            nc.gpsimd.memset(ones[:], 1.0).then_inc(consts_ready, 1)
            nc.gpsimd.memset(zero[:], 0.0).then_inc(zero_ready, 1)
            link(nc.gpsimd.memset(mhalf[:], -0.5))

            def inv_std(n):
                pool.wait_ge(mv_ready, n + 1)
                link(nc.gpsimd.tensor_scalar(veps[:, grp(n)], mv[:, grp(n), 1], EPS, None, ALU.add))
                nc.gpsimd.tensor_tensor(rstd[:, grp(n)], veps[:, grp(n)], mhalf[:], ALU.pow).then_inc(rstd_ready, 1)

            inv_std(0)
            inv_std(1)
            pool.wait_ge(w_in, 16)
            link(nc.gpsimd.tensor_copy(wj_hi[:], w[:, W_J:W_J + D]))
            nc.gpsimd.tensor_tensor(wj_lo[:], w[:, W_J:W_J + D], wj_hi[:].bitcast(F32), ALU.subtract).then_inc(wj_ready, 1)

            pool.wait_ge(zero_ready, 1)

            def mean_field(b):
                pool.wait_ge(sT_hi_ready, GB * (b + 1))
                link(nc.gpsimd.tensor_tensor(msum[:], ssum[:, 2 * b:2 * b + 1], ssum[:, 2 * b + 1:2 * b + 2], ALU.add))
                nc.gpsimd.tensor_scalar(meanb[:], zero[:], msum[:, 0:1], 1.0 / N,
                                        ALU.add, ALU.mult).then_inc(mean_ready, 1)

            def split_v(q):
                drained(pool, ("V", q))
                link(nc.gpsimd.tensor_copy(v_hi[:, grp(q), :], st[:, grp(q), :]))
                nc.gpsimd.tensor_tensor(v_lo[:, grp(q), :], st[:, grp(q), :], v_hi[:, grp(q), :].bitcast(F32),
                                        ALU.subtract).then_inc(v_ready, 1)

            def add_global(b):
                drained(pool, ("G", b))
                pool.wait_ge(v_ready, GB * (b + 1))
                rows = st[:, b * NT:(b + 1) * NT, :]
                nc.gpsimd.tensor_tensor(rows, rows, gb[:, b, :].unsqueeze(1).to_broadcast([P, NT, D]),
                                        ALU.add).then_inc(sg_ready, 1)

            def split_w13(e):
                pool.wait_ge(w13_in[e % 4], 16 * (e // 4 + 1))
                link(nc.gpsimd.tensor_copy(w13_hi[:, e, :], stage[:, e % 4, :]))
                nc.gpsimd.tensor_tensor(w13_lo[:, e, :], stage[:, e % 4, :], w13_hi[:, e, :].bitcast(F32),
                                        ALU.subtract).then_inc(w13_split, 1)

            def residual(g):
                pool.wait_ge(tanh_ready, g + 1)
                nc.gpsimd.tensor_tensor(xt[:, grp(g), :], xt[:, grp(g), :], arg[:, g % 2, :, :],
                                        ALU.add).then_inc(x1_ready, 1)

            def scatter(b):
                pool.wait_ge(slots_ready, b + 1)
                pool.wait_ge(xs_zeroed[b], 16)
                for t in range(NT):
                    for k in range(K):
                        nc.gpsimd.indirect_dma_start(
                            xs[b][:, :], bass.IndirectOffsetOnAxis(ap=slots[:, b, k, t:t + 1], axis=0),
                            xn[:, b * NT + t, :], None).then_inc(scattered[b], 16)

            def gather(b):
                for par in range(2):
                    pool.wait_ge(y_stored[par], 16 * (b + 1) * ST // QUAD)
                for t in range(NT):
                    for k in range(K):
                        nc.gpsimd.indirect_dma_start(
                            rows_of[b][:, k * NT + t, :], None, ys[b][:, :],
                            bass.IndirectOffsetOnAxis(ap=slots[:, b, k, t:t + 1], axis=0)).then_inc(gathered[b][t], 16)

            mean_field(0)
            split_w13(0)
            split_v(0)
            inv_std(2)
            split_v(1)
            inv_std(3)
            add_global(0)
            mean_field(1)
            split_w13(1)
            split_v(2)
            split_v(3)
            add_global(1)
            split_w13(2)
            split_w13(3)
            residual(0)
            split_w13(4)
            inv_std(GROUPS)
            residual(1)
            split_w13(5)
            inv_std(GROUPS + 1)
            split_w13(6)
            split_w13(7)
            scatter(0)
            inv_std(GROUPS + 2)
            inv_std(GROUPS + 3)
            scatter(1)
            gather(0)
            gather(1)

        @block.scalar
        def _(act):
            act.dma_start(c[:], cst).then_inc(c_in, 16)
            act.dma_start(w[:], wpack).then_inc(w_in, 16)
            act.wait_ge(c_in, 16)
            nc.scalar.copy(tri[:], c[:, C_TRI:C_TRI + P]).then_inc(consts_ready, 1)

            def evac_xT(q):
                wait_misc(act, ("xT", q))
                nc.scalar.copy(xnT[:, cols(q)], misc(("xT", q))).then_inc(bank_free(("xT", q)), 1)

            def evac_sT_hi(q):
                wait_misc(act, ("sT", q))
                nc.scalar.activation(sT_hi[:, cols(q)], misc(("sT", q)), ACT.Identity, bias=w[:, B_COL:B_COL + 1],
                                     accum_out=ssum[:, q:q + 1]).then_inc(sT_hi_ready, 1)

            def evac_e_hi(g):
                wait_misc(act, ("e", g))
                nc.scalar.activation(e_hi[:, g % 2, :], misc(("e", g)), ACT.Copy, scale=SCALE).then_inc(e_hi_ready, 1)

            def evac_G(b):
                wait_misc(act, ("G", b))
                nc.scalar.copy(gb[:, b, :], misc(("G", b))[:, 0:D]).then_inc(bank_free(("G", b)), 1)

            def softmax_exp(i):
                act.wait_ge(max_ready, i + 1)
                nc.scalar.activation(probs[:, i % 2, :], S[:, i % 2, :], ACT.Exp, bias=nmax[:, i:i + 1],
                                     accum_out=L[:, i:i + 1]).then_inc(probs_ready, 1)

            def evac_pT_hi(i):
                g, r = divmod(i, GT)
                for k in range(2):
                    act.wait_ge(PT_full, 2 * i + k + 1)
                    nc.scalar.copy(pT_hi[:, g % 2, 4 * k:4 * k + 4, r * P:(r + 1) * P],
                                   PT[:, k, :].rearrange("p (c n) -> p c n", c=4)).then_inc(pT_hi_ready, 1)

            def evac_oT(g):
                wait_misc(act, ("AV", g))
                nc.scalar.copy(oT, misc(("AV", g))).then_inc(bank_free(("AV", g)), 1)

            def tanh(g):
                drained(act, ("OT", g))
                nc.scalar.activation(arg[:, g % 2, :, :], arg[:, g % 2, :, :], ACT.Tanh,
                                     scale=w[:, BETA:BETA + 1]).then_inc(tanh_ready, 1)

            def evac_x2T(g):
                wait_misc(act, ("X2", g))
                nc.scalar.copy(x2T, misc(("X2", g))).then_inc(bank_free(("X2", g)), 1)

            def gate_softmax_exp(b):
                act.wait_ge(gate_sub, b + 1)
                nc.scalar.activation(r64[:, 1, :, :], r64[:, 0, :, :], ACT.Exp).then_inc(gate_exp, 1)

            def evacuate(kind, n):
                if kind == "xT":
                    evac_xT(n)
                elif kind == "sT":
                    evac_sT_hi(n)
                elif kind == "e":
                    evac_e_hi(n)
                elif kind == "G":
                    evac_G(n)
                elif kind == "X2":
                    evac_x2T(n)

            act.wait_ge(w_in, 16)
            for kind, n in START[:5]:
                evacuate(kind, n)
            softmax_exp(0)
            evac_G(0)
            for i in range(TILES):
                evac_pT_hi(i)
                for kind, n in BEFORE.get(i, []):
                    evacuate(kind, n)
                if i + 1 < TILES:
                    softmax_exp(i + 1)
                if i == 8:
                    tanh(0)
                if i == 9:
                    tanh(1)
                if i == 13:
                    gate_softmax_exp(0)
                for kind, n in AFTER.get(i, []):
                    evacuate(kind, n)
                if i in (7, 8):
                    evac_oT(i - 7)
            evac_oT(2)
            tanh(2)
            evac_oT(3)

            def silu(t, u):
                act.wait_ge(gu_full, t + 1)
                nc.scalar.activation(sg[:, u, :], S[:, 0, u * 2 * H:u * 2 * H + H], ACT.Silu).then_inc(silu_ready, 1)

            def slotT_hi(t, u):
                act.wait_ge(slotT_full, t + 1)
                nc.scalar.copy(gT_hi[:, u, :], PT[:, 0, u * P:(u + 1) * P]).then_inc(slotT_hi_ready, 1)

            def evac_hT(t, u):
                act.wait_ge(hT_full, t + 1)
                nc.scalar.copy(hT[:, u, :], PT[:, 1, u * H:(u + 1) * H]).then_inc(hT_ready, 1)

            slotT_hi(0, 0)
            slotT_hi(1, 1)
            tanh(3)
            silu(0, 0)
            slotT_hi(2, 0)
            for t in range(ROUND):
                if t >= 1:
                    evac_hT(t - 1, (t - 1) % 2)
                silu(t + 1, (t + 1) % 2)
                slotT_hi(t + 3, (t + 3) % 2)
                for kind, n in LATE.get(t, []):
                    evacuate(kind, n)
            with act.Fori(1, SLOT_TILES // ROUND - 1) as r:
                for v in range(ROUND):
                    evac_hT(r * ROUND + v - 1, (v + 1) % 2)
                    silu(r * ROUND + v + 1, (v + 1) % 2)
                    slotT_hi(r * ROUND + v + 3, (v + 1) % 2)
            for t in range(SLOT_TILES - ROUND, SLOT_TILES):
                evac_hT(t - 1, (t - 1) % 2)
                if t + 1 < SLOT_TILES:
                    silu(t + 1, (t + 1) % 2)
                if t + 3 < SLOT_TILES:
                    slotT_hi(t + 3, (t + 3) % 2)
            evac_hT(SLOT_TILES - 1, (SLOT_TILES - 1) % 2)
            gate_softmax_exp(1)

        @block.vector
        def _(dve):
            steps = [0]

            def link(ins):
                steps[0] += 1
                ins.then_inc(dve_step, 1)
                dve.wait_ge(dve_step, steps[0])

            def stats(n):
                for j in range(GT):
                    ins = nc.vector.bn_stats(bn[:, n % 2, j, :], xt[:, (n % GROUPS) * GT + j, :])
                link(ins)
                for j in range(GT):
                    ins = nc.vector.bn_aggr(mv[:, n * GT + j, :], bn[:, n % 2, j, :])
                ins.then_inc(mv_ready, 1)

            def normalise(n):
                dve.wait_ge(rstd_ready, n + 1)
                for j in range(GT):
                    i = (n % GROUPS) * GT + j
                    ins = nc.vector.tensor_scalar(xn[:, i, :], xt[:, i, :], mv[:, n * GT + j, 0:1],
                                                  rstd[:, n * GT + j:n * GT + j + 1], ALU.subtract, ALU.mult)
                ins.then_inc(xn_ready, 1)

            def evac_sT_lo(q):
                dve.wait_ge(sT_hi_ready, q + 1)
                nc.vector.scalar_tensor_tensor(out=sT_lo[:, cols(q)], in0=misc(("sT", q)), scalar=w[:, B_COL:B_COL + 1],
                                               in1=sT_hi[:, cols(q)].bitcast(F32), op0=ALU.add,
                                               op1=ALU.subtract).then_inc(bank_free(("sT", q)), 1)

            def evac_e_lo(g):
                dve.wait_ge(e_hi_ready, g + 1)
                nc.vector.scalar_tensor_tensor(out=e_lo[:, g % 2, :], in0=misc(("e", g)), scalar=SCALE,
                                               in1=e_hi[:, g % 2, :].bitcast(F32), op0=ALU.mult,
                                               op1=ALU.subtract).then_inc(bank_free(("e", g)), 1)

            def evac_s(q):
                wait_misc(dve, ("V", q))
                ins = nc.vector.tensor_tensor(st[:, grp(q), :], misc(("V", q)).rearrange("p (t d) -> p t d", t=GT),
                                              w[:, B_ROW:B_ROW + D].unsqueeze(1).to_broadcast([P, GT, D]), ALU.add)
                ins.then_inc(bank_free(("V", q)), 1)

            def row_max(i):
                dve.wait_ge(S_full, i + 1)
                nc.vector.tensor_reduce(nmax[:, i:i + 1], S[:, i % 2, :], AXX, ALU.max, negate=True).then_inc(max_ready, 1)

            def evac_pT_lo(i):
                g, r = divmod(i, GT)
                for k in range(2):
                    dve.wait_ge(pT_hi_ready, 2 * i + k + 1)
                    part = (slice(None), g % 2, slice(4 * k, 4 * k + 4), slice(r * P, (r + 1) * P))
                    nc.vector.tensor_tensor(pT_lo[part], PT[:, k, :].rearrange("p (c n) -> p c n", c=4),
                                            pT_hi[part].bitcast(F32), ALU.subtract).then_inc(pT_ready, 1)

            def tanh_arg(g):
                link(nc.vector.reciprocal(rL[:, grp(g)], L[:, grp(g)]))
                wait_misc(dve, ("OT", g))
                dve.wait_ge(sg_ready, g // GB + 1)
                for j in range(GT):
                    i = g * GT + j
                    ins = nc.vector.scalar_tensor_tensor(out=arg[:, g % 2, j, :], in0=misc(("OT", g))[:, j * P:(j + 1) * P],
                                                         scalar=rL[:, i:i + 1], in1=st[:, i, :], op0=ALU.mult, op1=ALU.add)
                ins.then_inc(bank_free(("OT", g)), 1)

            def residual(g):
                dve.wait_ge(tanh_ready, g + 1)
                link(nc.vector.tensor_tensor(xt[:, grp(g), :], xt[:, grp(g), :], arg[:, g % 2, :, :], ALU.add))

            def stats_after(g):
                dve.wait_ge(x1_ready, g + 1)
                stats(GROUPS + g)

            def take_logits(g):
                wait_misc(dve, ("LG", g))
                nc.vector.tensor_copy(lg[:, grp(g), :], misc(("LG", g))[:, 0:GT * E].rearrange("p (t e) -> p t e", e=E)
                                      ).then_inc(bank_free(("LG", g)), 1)

            def col(n):
                return r8[:, n, :]

            def bc(ap):
                return ap.unsqueeze(2).to_broadcast([P, NT, E])

            def gate_max(b):
                drained(dve, ("LG", GB * b + 1))
                rows = lg[:, b * NT:(b + 1) * NT, :]
                link(nc.vector.tensor_reduce(col(0), rows, AXX, ALU.max))
                nc.vector.tensor_tensor(r64[:, 0, :, :], rows, bc(col(0)), ALU.subtract).then_inc(gate_sub, 1)

            def choose(b):
                less_max = r64[:, 0, :, :]
                desc = c[:, C_DESC:C_DESC + E].unsqueeze(1).to_broadcast([P, NT, E])
                dve.wait_ge(gate_sub, b + 1)
                link(nc.vector.scalar_tensor_tensor(out=r64[:, 2, :, :], in0=less_max, scalar=0.0, in1=desc,
                                                    op0=ALU.is_equal, op1=ALU.mult))
                link(nc.vector.tensor_reduce(col(1), r64[:, 2, :, :], AXX, ALU.max))
                link(nc.vector.tensor_tensor(hot[:, 0, :, :], r64[:, 2, :, :], bc(col(1)), ALU.is_equal))
                link(nc.vector.scalar_tensor_tensor(out=r64[:, 3, :, :], in0=hot[:, 0, :, :], scalar=-3e38,
                                                    in1=less_max, op0=ALU.mult, op1=ALU.min))
                link(nc.vector.tensor_reduce(col(2), r64[:, 3, :, :], AXX, ALU.max))
                link(nc.vector.tensor_tensor(r64[:, 2, :, :], r64[:, 3, :, :], bc(col(2)), ALU.is_equal))
                link(nc.vector.tensor_tensor(r64[:, 4, :, :], r64[:, 2, :, :], desc, ALU.mult))
                link(nc.vector.tensor_reduce(col(3), r64[:, 4, :, :], AXX, ALU.max))
                link(nc.vector.tensor_tensor(hot[:, 1, :, :], r64[:, 4, :, :], bc(col(3)), ALU.is_equal))
                nc.vector.tensor_tensor(sel[:], hot[:, 0, :, :], hot[:, 1, :, :], ALU.add).then_inc(sel_ready, 1)

            def gate_values(b):
                dve.wait_ge(gate_exp, b + 1)
                ex = r64[:, 1, :, :]
                link(nc.vector.tensor_reduce(col(4), ex, AXX, ALU.add))
                link(nc.vector.reciprocal(col(5), col(4)))
                link(nc.vector.tensor_tensor(prod, hot[:], ex.unsqueeze(1).to_broadcast([P, K, NT, E]), ALU.mult))
                link(nc.vector.tensor_reduce(slotf[:], prod, AXX, ALU.add))
                link(nc.vector.tensor_tensor(gate[:, b, :, :], slotf[:],
                                             col(5).unsqueeze(1).to_broadcast([P, K, NT]), ALU.mult))

            def place(b):
                wait_misc(dve, ("R", b))
                dve.wait_ge(sg_ready, NB)
                rank = misc(("R", b))[:, 0:NT * E].rearrange("p (t e) -> p t e", e=E)
                count = misc(("R", b))[:, NT * E:NT * E + E]
                thr = c[:, C_THR:C_THR + N // P].unsqueeze(1).to_broadcast([P, E, N // P])
                link(nc.vector.tensor_tensor(cmp[:], count.unsqueeze(2).to_broadcast([P, E, N // P]), thr, ALU.is_gt))
                link(nc.vector.tensor_reduce(tiles_e[:], cmp[:], AXX, ALU.add))
                link(nc.vector.tensor_tensor(cmp[:], tiles_e[:].unsqueeze(1).to_broadcast([P, E, E]),
                                             c[:, C_LT:C_LT + E * E].rearrange("p (e f) -> p e f", f=E), ALU.mult))
                link(nc.vector.tensor_reduce(base[:], cmp[:], AXX, ALU.add))
                link(nc.vector.tensor_tensor(ends[:], base[:], tiles_e[:], ALU.add))
                link(nc.vector.tensor_tensor(cmpj, ends[0:1, :].unsqueeze(1).to_broadcast([1, ST, E]),
                                             c[0:1, C_J:C_J + ST].unsqueeze(2).to_broadcast([1, ST, E]), ALU.is_le))
                link(nc.vector.tensor_reduce(tabf[:], cmpj, AXX, ALU.add))
                link(nc.vector.tensor_scalar(tab[:, b * ST:(b + 1) * ST], tabf[:], float(E - 1), None, ALU.min))
                nc.vector.scalar_tensor_tensor(out=r64[:, 4, :, :], in0=base[:].unsqueeze(1).to_broadcast([P, NT, E]),
                                               scalar=float(P), in1=rank, op0=ALU.mult,
                                               op1=ALU.add).then_inc(bank_free(("R", b)), 1)
                drained(dve, ("R", b))
                link(nc.vector.tensor_tensor(prod, hot[:], r64[:, 4, :, :].unsqueeze(1).to_broadcast([P, K, NT, E]),
                                             ALU.mult))
                link(nc.vector.tensor_reduce(slotf[:], prod, AXX, ALU.add))
                ins = nc.vector.tensor_scalar(slots[:, b, :, :], slotf[:], float(ST * P - 1), None, ALU.min)
                ins.then_inc(slots_ready, 1)

            def combine(b):
                for t in range(NT):
                    i = b * NT + t
                    dve.wait_ge(gathered[b][t], 16 * K)
                    for k in range(K):
                        ins = nc.vector.scalar_tensor_tensor(out=xt[:, i, :], in0=rows_of[b][:, k * NT + t, :],
                                                             scalar=gate[:, b, k, t:t + 1], in1=xt[:, i, :],
                                                             op0=ALU.mult, op1=ALU.add)
                        if k == 0:
                            link(ins)
                    ins.then_inc(out_ready, 1)

            for q in range(2):
                dve.wait_ge(x_in[q], 16)
                stats(q)
            normalise(0)
            normalise(1)
            dve.wait_ge(w_in, 16)

            def evacuate(kind, n):
                if kind == "sT":
                    evac_sT_lo(n)
                elif kind == "e":
                    evac_e_lo(n)
                elif kind == "V":
                    evac_s(n)
                elif kind == "OT":
                    tanh_arg(n)
                elif kind == "LG":
                    take_logits(n)

            for kind, n in START[:5]:
                evacuate(kind, n)
            row_max(0)
            row_max(1)
            evac_s(0)
            evac_s(1)
            for i in range(TILES):
                evac_pT_lo(i)
                for kind, n in BEFORE.get(i, []):
                    evacuate(kind, n)
                if i + 2 < TILES:
                    row_max(i + 2)
                for kind, n in AFTER.get(i, []):
                    evacuate(kind, n)
                if i == 0:
                    dve.wait_ge(x_in[2], 16)
                    stats(2)
                if i == 1:
                    normalise(2)
                    stats(3)
                if i == 2:
                    normalise(3)
                if i == 8:
                    stats_after(0)
                if i == 9:
                    normalise(GROUPS)
                    stats_after(1)
                if i == 10:
                    normalise(GROUPS + 1)
                if i == 11:
                    gate_max(0)
                    choose(0)
                if i == 12:
                    place(0)
                    gate_values(0)
            residual(2)
            stats(GROUPS + 2)

            def hidden(t, u):
                dve.wait_ge(silu_ready, t + 1)
                nc.vector.tensor_tensor(h[:, u, :], sg[:, u, :], S[:, 0, u * 2 * H + H:(u + 1) * 2 * H],
                                        ALU.mult).then_inc(h_ready, 1)

            def slotT_lo(t, u):
                dve.wait_ge(slotT_hi_ready, t + 1)
                nc.vector.tensor_tensor(gT_lo[:, u, :], PT[:, 0, u * P:(u + 1) * P], gT_hi[:, u, :].bitcast(F32),
                                        ALU.subtract).then_inc(slotT_ready, 1)

            def evac_y(t, v, stored):
                dve.wait_ge(y_full, t + 1)
                if stored is not None and v % 2 == 0:
                    dve.wait_ge(y_stored[v // 2], 16 * stored)
                nc.vector.tensor_copy(y[:, v, :], S[:, 1, (v % 2) * GW:(v % 2) * GW + D]).then_inc(y_ready, 1)

            slotT_lo(0, 0)
            slotT_lo(1, 1)
            tanh_arg(3)
            hidden(0, 0)
            slotT_lo(2, 0)
            normalise(GROUPS + 2)

            def tile_step(t, v, stored, output=True):
                if output:
                    evac_y(t - 2, (v + 2) % 4, stored)
                hidden(t + 1, (v + 1) % 2)
                slotT_lo(t + 3, (v + 1) % 2)

            for t in range(ROUND):
                tile_step(t, t % QUAD, (t - 2) // QUAD if t >= 6 else None, output=t >= 2)
                for kind, n in LATE.get(t, []):
                    evacuate(kind, n)
                if t == 0:
                    residual(3)
                    stats(GROUPS + 3)
                if t == 2:
                    normalise(GROUPS + 3)
                if t == 4:
                    gate_max(1)
                    choose(1)
                if t == 6:
                    place(1)
            with dve.Fori(1, SLOT_TILES // ROUND - 1) as r:
                for v in range(ROUND):
                    tile_step(r * ROUND + v, v % QUAD, 2 * r + (v - 2) // QUAD)
            for t in range(SLOT_TILES - ROUND, SLOT_TILES):
                v = t % QUAD
                evac_y(t - 2, (v + 2) % 4, (t - 2) // 4)
                if t + 1 < SLOT_TILES:
                    hidden(t + 1, (v + 1) % 2)
                if t + 3 < SLOT_TILES:
                    slotT_lo(t + 3, (v + 1) % 2)
            for t in range(SLOT_TILES - 2, SLOT_TILES):
                evac_y(t, t % 4, t // 4)
            combine(0)
            gate_values(1)
            combine(1)

        @block.tensor
        def _(pe):
            def take(use):
                k, turn = MISC[use]
                if turn > 0:
                    pe.wait_ge(misc_free[k], turn)

            def matmul3(dst, w_hi, w_lo, m_hi, m_lo, start, stop):
                pe.matmul(dst, w_hi, m_hi, start=start, stop=False)
                pe.matmul(dst, w_hi, m_lo, start=False, stop=False)
                return pe.matmul(dst, w_lo, m_hi, start=False, stop=stop)

            def transposes(use, src):
                take(use)
                for j in range(GT):
                    ins = pe.transpose(misc(use)[:, j * P:(j + 1) * P], src(j), ident)
                ins.then_inc(misc_full[MISC[use][0]], 1)

            def xT(q):
                pe.wait_ge(xn_ready, q + 1)
                transposes(("xT", q), lambda j: xn[:, q * GT + j, :])

            def sT(q):
                use = ("sT", q)
                take(use)
                drained(pe, ("xT", q))
                pe.matmul(misc(use), w[:, W_SPIN:W_SPIN + D], xnT[:, cols(q)], start=True,
                          stop=True).then_inc(misc_full[MISC[use][0]], 1)

            def V(q):
                use = ("V", q)
                take(use)
                for j in range(GT):
                    i = q * GT + j
                    ins = pe.matmul(misc(use)[:, j * P:(j + 1) * P], xnT[:, i * P:(i + 1) * P],
                                    w[:, W_SPIN:W_SPIN + D], start=True, stop=True)
                ins.then_inc(misc_full[MISC[use][0]], 1)

            def G(b):
                use = ("G", b)
                take(use)
                pe.wait_ge(mean_ready, b + 1)
                pe.matmul(misc(use)[:, 0:D], meanb[:], w[:, W_GLOB:W_GLOB + D], start=True,
                          stop=True).then_inc(misc_full[MISC[use][0]], 1)

            def energies(g):
                use = ("e", g)
                take(use)
                if g == 0:
                    pe.wait_ge(wj_ready, 1)
                drained(pe, ("sT", g))
                matmul3(misc(use), wj_hi[:], wj_lo[:], sT_hi[:, cols(g)], sT_lo[:, cols(g)], True,
                        True).then_inc(misc_full[MISC[use][0]], 1)

            def scores_of(i):
                g, r = divmod(i, GT)
                b = i // NT
                if r == 0:
                    drained(pe, ("e", g))
                q = slice(r * P, (r + 1) * P)
                for k in range(GB):
                    ins = matmul3(S[:, i % 2, k * GW:(k + 1) * GW], e_hi[:, g % 2, q], e_lo[:, g % 2, q],
                                  sT_hi[:, cols(GB * b + k)], sT_lo[:, cols(GB * b + k)], True, True)
                ins.then_inc(S_full, 1)

            def transpose_probs(i):
                pe.wait_ge(probs_ready, i + 1)
                for k in range(2):
                    if i > 0:
                        pe.wait_ge(pT_ready, 2 * (i - 1) + k + 1)
                    for m in range(4):
                        ch = 4 * k + m
                        ins = pe.transpose(PT[:, k, m * P:(m + 1) * P], probs[:, i % 2, ch * P:(ch + 1) * P], ident)
                    ins.then_inc(PT_full, 1)

            def AV(g, share, shares):
                use = ("AV", g)
                b = g // GB
                if share == 0:
                    take(use)
                    pe.wait_ge(v_ready, GB * (b + 1))
                    pe.wait_ge(pT_ready, 2 * GT * (g + 1))
                for ch in range(share * CH // shares, (share + 1) * CH // shares):
                    i = b * NT + ch
                    ins = matmul3(misc(use), v_hi[:, i, :], v_lo[:, i, :], pT_hi[:, g % 2, ch, :],
                                  pT_lo[:, g % 2, ch, :], ch == 0, ch == CH - 1)
                if share == shares - 1:
                    ins.then_inc(misc_full[MISC[use][0]], 1)

            def OT(g):
                drained(pe, ("AV", g))
                transposes(("OT", g), lambda j: oT[:, j * P:(j + 1) * P])

            def X2(g):
                pe.wait_ge(xn_ready, GROUPS + g + 1)
                transposes(("X2", g), lambda j: xn[:, g * GT + j, :])

            def LG(g):
                use = ("LG", g)
                take(use)
                drained(pe, ("X2", g))
                for j in range(GT):
                    ins = pe.matmul(misc(use)[:, j * E:(j + 1) * E], x2T[:, j * P:(j + 1) * P],
                                    w[:, W_GATE:W_GATE + E], start=True, stop=True)
                ins.then_inc(misc_full[MISC[use][0]], 1)

            def R(b):
                use = ("R", b)
                take(use)
                pe.wait_ge(sel_ready, b + 1)
                bank = misc(use)
                rank = bank[:, 0:NT * E].rearrange("p (t e) -> p t e", e=E)
                pe.matmul(rank, tri[:], sel[:], start=True, stop=True, skip_group_check=True)
                for t in range(NT - 1):
                    pe.matmul(rank[:, t + 1:NT, :], ones[:], sel[:, t:t + 1, :].to_broadcast([P, NT - 1 - t, E]),
                              start=False, stop=True, skip_group_check=True)
                for t in range(NT):
                    ins = pe.matmul(bank[:, NT * E:NT * E + E], ones[:], sel[:, t, :], start=(t == 0),
                                    stop=(t == NT - 1))
                ins.then_inc(misc_full[MISC[use][0]], 1)

            pe.wait_ge(c_in, 16)
            pe.wait_ge(w_in, 16)
            shares_done = {g: 0 for g in range(GROUPS)}

            def do(kind, n):
                if kind == "AV":
                    AV(n, shares_done[n], ORDER.count((kind, n)))
                    shares_done[n] += 1
                else:
                    {"xT": xT, "sT": sT, "e": energies, "V": V, "G": G, "OT": OT, "X2": X2, "LG": LG, "R": R}[kind](n)

            for kind, n in START[:5]:
                do(kind, n)
            scores_of(0)
            scores_of(1)
            for kind, n in START[5:]:
                do(kind, n)
            pe.wait_ge(consts_ready, 2)
            for i in range(TILES):
                transpose_probs(i)
                for kind, n in BEFORE.get(i, []):
                    do(kind, n)
                if i + 2 < TILES:
                    scores_of(i + 2)
                for kind, n in AFTER.get(i, []):
                    do(kind, n)
            def experts_of(first, n):
                _, e = nc.values_load_multi_w_load_instructions(
                    tab[0:1, bass.ds(first, n)], engines=[mybir.EngineType.PE], min_val=0, max_val=E - 1,
                    skip_runtime_bounds_check_because="the table is cut off at the last expert")
                return e

            def slotT(t, v, loads):
                if v % 2 == 0:
                    pe.wait_ge(slot_loaded[v // 2], 16 * loads)
                if not (isinstance(t, int) and t == 0):
                    pe.wait_ge(slotT_ready, t)
                u = v % 2
                pe.transpose(PT[:, 0, u * P:(u + 1) * P], xs_in[:, v, :], ident).then_inc(slotT_full, 1)

            def gate_up(t, u, e, taken):
                pe.wait_ge(slotT_ready, t + 1)
                if taken is not None:
                    pe.wait_ge(h_ready, taken)
                bank = S[:, 0, u * 2 * H:(u + 1) * 2 * H]
                hi, lo = [a[:, bass.ds(e, 1), :].rearrange("p a n -> p (a n)") for a in (w13_hi, w13_lo)]
                pe.matmul(bank, gT_hi[:, u, :], hi, start=True, stop=False)
                pe.matmul(bank, gT_lo[:, u, :], hi, start=False, stop=False)
                pe.matmul(bank, gT_hi[:, u, :], lo, start=False, stop=True).then_inc(gu_full, 1)

            def hiddenT(t, u):
                pe.wait_ge(h_ready, t + 1)
                for k in range(2):
                    ins = pe.transpose(PT[:, 1, u * H + k * P:u * H + (k + 1) * P], h[:, u, k * P:(k + 1) * P], ident)
                ins.then_inc(hT_full, 1)

            def down(t, u, e, taken):
                pe.wait_ge(hT_ready, t + 1)
                if taken is not None:
                    pe.wait_ge(y_ready, taken)
                for k in range(2):
                    ins = pe.matmul(S[:, 1, u * GW:u * GW + D], hT[:, u, k * P:(k + 1) * P],
                                    w2s[:, bass.ds(e, 1), k, :].rearrange("p a n -> p (a n)"), start=(k == 0), stop=(k == 1))
                ins.then_inc(y_full, 1)

            pe.wait_ge(w13_split, E)
            pe.wait_ge(w2_in, 16)
            slotT(0, 0, 1)
            slotT(1, 1, 1)
            ex = experts_of(0, ROUND + 1)
            do("OT", 3)
            gate_up(0, 0, ex[0], None)
            slotT(2, 2, 1)
            for t in range(ROUND):
                if t >= 2:
                    down(t - 2, t % 2, ex[t - 2], t - 3 if t > 3 else None)
                if t >= 1:
                    hiddenT(t - 1, (t - 1) % 2)
                gate_up(t + 1, (t + 1) % 2, ex[t + 1], t if t >= 1 else None)
                slotT(t + 3, (t + 3) % ROUND, (t + 3) // ROUND + 1)
                for kind, n in LATE.get(t, []):
                    do(kind, n)
            with pe.Fori(1, SLOT_TILES // ROUND - 1) as r:
                ex = experts_of(r * ROUND - 2, ROUND + 3)
                for v in range(ROUND):
                    t = r * ROUND + v
                    down(t - 2, v % 2, ex[v], t - 3)
                    hiddenT(t - 1, (v + 1) % 2)
                    gate_up(t + 1, (v + 1) % 2, ex[v + 3], t)
                    slotT(t + 3, (v + 3) % ROUND, r + 1 + (v + 3) // ROUND)
            last = SLOT_TILES - ROUND
            ex = experts_of(last - 2, ROUND + 2)
            for t in range(last, SLOT_TILES):
                down(t - 2, t % 2, ex[t - last], t - 3)
                hiddenT(t - 1, (t - 1) % 2)
                if t + 1 < SLOT_TILES:
                    gate_up(t + 1, (t + 1) % 2, ex[t - last + 3], t)
                if t + 3 < SLOT_TILES:
                    slotT(t + 3, (t + 3) % ROUND, (t + 3) // ROUND + 1)
            down(SLOT_TILES - 2, 0, ex[ROUND], SLOT_TILES - 3)
            hiddenT(SLOT_TILES - 1, 1)
            down(SLOT_TILES - 1, 1, ex[ROUND + 1], SLOT_TILES - 2)


def kernel(L0_attn_x, L0_attn_W_spin, L0_attn_b_spin, L0_attn_W_global, L0_attn_W_J, L0_attn_beta,
           L0_ffn_gate_w, L0_ffn_w1, L0_ffn_w2, L0_ffn_w3):
    import concourse.bacc as bacc
    from concourse.bass_utils import run_bass_kernel_spmd

    b = np.asarray(L0_attn_b_spin)
    wpack = np.concatenate([
        np.asarray(L0_attn_W_spin).T, np.asarray(L0_attn_W_J).T, np.asarray(L0_attn_W_global).T,
        np.broadcast_to(b[None, :], (P, D)), np.asarray(L0_ffn_gate_w).T, b[:, None],
        np.broadcast_to(np.asarray(L0_attn_beta)[None, :], (P, 1))], axis=1)
    w13 = np.concatenate([np.asarray(L0_ffn_w1), np.asarray(L0_ffn_w3)], axis=2).transpose(1, 0, 2)
    w2 = np.asarray(L0_ffn_w2).reshape(E, 2, P, D).transpose(2, 0, 1, 3)
    arrays = {"x": np.asarray(L0_attn_x), "wpack": wpack, "cst": constants(), "w13": w13, "w2": w2}
    arrays = {k: np.ascontiguousarray(v) for k, v in arrays.items()}

    nc = bacc.Bacc("TRN2", target_bir_lowering=False, num_devices=1)
    ins = [nc.dram_tensor(k, v.shape, F32, kind="ExternalInput").ap() for k, v in arrays.items()]
    xs = [nc.dram_tensor(f"xs{i}", (ST * P, D), F32).ap() for i in range(NB)]
    ys = [nc.dram_tensor(f"ys{i}", (ST * P, D), F32).ap() for i in range(NB)]
    out = nc.dram_tensor("out", (NB, N, D), F32, kind="ExternalOutput").ap()
    build(nc, *ins, xs, ys, out)
    r = run_bass_kernel_spmd(nc, [arrays], core_ids=[0])
    return r.results[0]["out"]
```

```python
from contextlib import ExitStack

import numpy as np

import concourse.bass as bass
from concourse import mybir

ALU = mybir.AluOpType
ACT = mybir.ActivationFunctionType
AXX = mybir.AxisListType.X
F32 = mybir.dt.float32
F32R = mybir.dt.float32r
BF16 = mybir.dt.bfloat16
U32 = mybir.dt.uint32
I32 = mybir.dt.int32

P = 128
D = 128
E = 8
H = 256
K = 2
NB = 2
N = 1024
NT = N // P
TILES = NB * NT
GT = 4
GW = GT * P
GROUPS = TILES // GT
GB = NT // GT
CH = N // P
SHARES = CH
EPS = 1e-5
SCALE = float(D) ** -0.5
ST = K * N // P + E - 1
SLOT_TILES = NB * ST
XR = D + 1
CHUNKS = [(0, 4), (4, 10), (10, ST)]
HALF = 12
WARM_UP = 17
STAY_WARM = 10
Y_PLACES = 26
QUAD = 4
BATCH = 15
PEELED = 2 * QUAD
LAST = (SLOT_TILES // QUAD - 1) * QUAD

W_SPIN, W_J, W_GLOB, B_ROW, W_GATE, B_COL, BETA, W_COLS = 0, 128, 256, 384, 512, 520, 521, 522
C_ID, C_TRI, C_DESC, C_LT, C_DEST, C_EMPTY, C_J = 0, 128, 256, 264, 328, 344, 344 + ST
C_COLS = C_J + ST


def constants():
    c = np.zeros((P, C_COLS), np.float32)
    c[:, C_ID:C_ID + P] = np.eye(P)
    c[:, C_TRI:C_TRI + P] = np.triu(np.ones((P, P)), 1)
    c[:, C_DESC:C_DESC + E] = np.arange(E, 0, -1)
    c[:, C_LT:C_LT + E * E] = np.tril(np.ones((E, E)), -1).reshape(-1)
    k, t = np.arange(K)[None, :, None], np.arange(NT)[None, None, :]
    c[:, C_DEST:C_DEST + K * NT] = (ST * P + k * N + np.arange(P)[:, None, None] * NT + t).reshape(P, K * NT)
    c[:, C_EMPTY:C_EMPTY + ST] = np.arange(ST) * P + np.arange(P)[:, None]
    c[:, C_J:C_J + ST] = np.arange(ST)
    return c


START = [("xT", 0), ("xT", 1), ("sT", 0), ("sT", 1), ("e", 0), ("V", 0), ("V", 1), ("G", 0)]
BEFORE = {1: [("e", 1), ("xT", 2)], 2: [("xT", 3)], 3: [("V", 3)], 4: [("G", 1)], 5: [("e", 2)], 6: [("e", 3)],
          7: [("OT", 0)], 8: [("OT", 1)], 9: [("LG", 0)], 14: [("OT", 2)]}
AFTER = {1: [("sT", 2)], 2: [("sT", 3)], 3: [("V", 2)],
         4: 3 * [("AV", 0)], 5: 3 * [("AV", 0)], 6: 2 * [("AV", 0)] + [("AV", 1)], 7: 7 * [("AV", 1)],
         8: [("X2", 0)], 10: [("X2", 1), ("AV", 2), ("LG", 1)], 11: 2 * [("AV", 2)] + [("R", 0), ("AV", 2)],
         12: 2 * [("AV", 2)], 13: 2 * [("AV", 2)], 14: 2 * [("AV", 3)], 15: 6 * [("AV", 3)]}
EARLY = [("OT", 3), ("X2", 2), ("LG", 2)]
MIDDLE = [("X2", 3)]
LATE = {0: [("LG", 3)], 2: [("R", 1)]}
ORDER = (START + [use for i in range(TILES) for use in BEFORE.get(i, []) + AFTER.get(i, [])] + EARLY + MIDDLE +
         [use for t in sorted(LATE) for use in LATE[t]])


def banks():
    place, turns, last, summing = {}, [0, 0], 1, None
    for n, use in enumerate(ORDER):
        if use not in place:
            last = 1 - (last if summing is None else summing)
            place[use] = (last, turns[last])
            turns[last] += 1
        if use[0] == "AV":
            summing = place[use][0] if use in ORDER[n + 1:] else None
            last = place[use][0]
    return place


MISC = banks()


def build(nc, x, wpack, cst, w13, w2, xs, placed, out):
    ctx = ExitStack()
    with ctx:
        def sb(name, shape, dt=F32):
            return ctx.enter_context(nc.sbuf_tensor(name, shape, dt))

        def sem(name):
            return ctx.enter_context(nc.semaphore(name))

        xt = sb("x_tokens", [P, TILES, D])
        xn = sb("x_normed", [P, TILES, XR])
        xnT = sb("x_normed_T", [P, TILES * P + NT])
        sT_hi = sb("sT_hi", [P, TILES * P], F32R)
        sT_lo = sb("sT_lo", [P, TILES * P], F32R)
        e_hi = sb("e_hi", [P, 2, GW], F32R)
        e_lo = sb("e_lo", [P, 2, GW], F32R)
        st = sb("s_tokens", [P, TILES, D])
        v_hi = sb("v_hi", [P, TILES, D], F32R)
        v_lo = sb("v_lo", [P, TILES, D], F32R)
        work = sb("probs_and_stage", [P, 2 * N + 4 * 2 * H])
        probs = work[:, 0:2 * N].rearrange("p (u n) -> p u n", u=2)
        stage = work[:, 2 * N:].rearrange("p (u n) -> p u n", u=4)
        pT_hi = sb("pT_hi", [P, 2, CH, GW], F32R)
        pT_lo = sb("pT_lo", [P, 2, CH, GW], F32R)
        arg_and_again = sb("tanh_arg_and_rows", [P, NT * XR])
        arg = arg_and_again[:].rearrange("p (g n) -> p g n", g=2)[:, :, 0:GW].rearrange("p g (t d) -> p g t d", d=D)
        w = sb("w_packed", [P, W_COLS])
        c = sb("constants", [P, C_COLS])
        tri = sb("tri_bf", [P, P], BF16)
        ones = sb("ones_bf", [P, P], BF16)
        wj_hi = sb("wj_hi", [P, D], F32R)
        wj_lo = sb("wj_lo", [P, D], F32R)
        w13_hi = sb("w13_hi", [P, E, 2 * H], F32R)
        w13_lo = sb("w13_lo", [P, E, 2 * H], F32R)
        w2s = sb("w2_rows", [P, E, 2, D])
        zero = sb("zero", [P, XR])
        bn = sb("bn_stats", [P, 2, GT, 6])
        mv = sb("mean_var", [P, TILES, 2])
        rstd = sb("rstd", [P, TILES])
        mhalf = sb("minus_half", [P, GT])
        ssum = sb("s_sums", [P, GROUPS])
        msum = sb("s_sum", [P, 1])
        meanb = sb("mean_bcast", [P, P])
        gb = sb("global_influence", [P, NB, D])
        nmax = sb("neg_max", [P, TILES])
        L = sb("exp_sums", [P, TILES])
        lg = sb("logits", [P, TILES, E])
        r8 = sb("route_cols", [P, 6, NT])
        r64 = sb("route_rows", [P, 6, NT, E])
        hot = sb("chosen", [P, K, NT, E])
        sel = sb("selected_bf", [P, NT, E], BF16)
        gate = sb("gate_values", [P, NB, K, NT])
        cmp = sb("compare", [P, E, E])
        tiles_e = sb("tiles_of_expert", [P, E])
        base = sb("first_tile", [P, E])
        ends = sb("end_tile", [P, E])
        slotf = sb("slots_f", [P, K, NT])
        slots = sb("slots", [P, NB, K, NT], U32)
        dest = sb("output_rows", [P, SLOT_TILES], U32)
        tab = sb("tile_expert", [1, SLOT_TILES], I32)

        oT = xnT[:, 0:GW]
        x2T = xnT[:, GW:2 * GW]
        lo_of = [pT_lo[:, k, :, :].rearrange("p c n -> p (c n)").bitcast(F32) for k in range(2)]
        rows_in = [a[:, 0:ST * XR].rearrange("p (t d) -> p t d", d=XR) for a in lo_of]
        xn_again = [a.rearrange("p (t d) -> p t d", d=XR) for a in (xnT[:, 2 * GW:], arg_and_again[:])]
        y = work[:, 2 * H:2 * H + Y_PLACES * D].rearrange("p (t d) -> p t d", d=D)
        gb_row = gb[0:1, :, :].rearrange("p b d -> p (b d)")
        cmpj = gb_row[:, 0:ST * E].rearrange("p (j e) -> p j e", e=E)
        tabf = gb_row[:, ST * E:ST * (E + 1)]
        prod = meanb[:].rearrange("p (k t e) -> p k t e", k=K, e=E)
        sg = xnT[:, 2 * GW:2 * GW + 2 * H].rearrange("p (u n) -> p u n", u=2)
        h = xnT[:, 3 * GW:3 * GW + 2 * H].rearrange("p (u n) -> p u n", u=2)
        gT_hi = e_hi[:, :, 0:P]
        gT_lo = e_lo[:, :, 0:P]
        hT = work[:, 0:2 * H].rearrange("p (u n) -> p u n", u=2)
        rows_of = [a.rearrange("p (k t d) -> p k t d", k=K, d=D)
                   for a in (st[:].rearrange("p t d -> p (t d)"), sT_hi[:].bitcast(F32))]

        second = rows_of[0][:, 0, :, :]

        ident = c[:, C_ID:C_ID + P]

        S = ctx.enter_context(nc.psum_tensor("S", [P, 2, N], F32))
        PT = ctx.enter_context(nc.psum_tensor("PT", [P, 2, GW], F32))
        MI = ctx.enter_context(nc.psum_tensor("MI", [P, 2, GW], F32))

        x_in = [sem(f"x_in{q}") for q in range(3)]
        w_in = sem("w_in")
        c_in = sem("c_in")
        w2_in = sem("w2_in")
        w13_in = [sem(f"w13_in{k}") for k in range(4)]
        w13_split = sem("w13_split")
        ones_ready = sem("ones_ready")
        tri_ready = sem("tri_ready")
        wj_ready = sem("wj_ready")
        zero_ready = sem("zero_ready")
        xs_zeroed = [sem(f"xs_zeroed{b}") for b in range(NB)]
        mv_ready = sem("mv_ready")
        rstd_ready = sem("rstd_ready")
        xn_ready = sem("xn_ready")
        misc_full = [sem(f"misc_full{k}") for k in range(2)]
        misc_free = [sem(f"misc_free{k}") for k in range(2)]
        sT_hi_ready = sem("sT_hi_ready")
        e_hi_ready = sem("e_hi_ready")
        mean_ready = sem("mean_ready")
        v_ready = sem("v_ready")
        sg_ready = sem("sG_ready")
        S_full = sem("S_full")
        max_ready = sem("max_ready")
        probs_ready = sem("probs_ready")
        PT_full = sem("PT_full")
        pT_hi_ready = sem("pT_hi_ready")
        pT_ready = sem("pT_ready")
        tanh_ready = sem("tanh_ready")
        x1_ready = sem("x1_ready")
        gate_sub = sem("gate_sub")
        gate_exp = sem("gate_exp")
        sel_ready = sem("sel_ready")
        slots_ready = sem("slots_ready")
        table_ready = sem("table_ready")
        scattered = [sem(f"scattered{b}") for b in range(NB)]
        dve_step = sem("dve_step")
        pool_step = sem("pool_step")
        again_ready = sem("again_ready")
        rows_loaded = [[sem(f"rows_loaded{b}_{k}") for k in range(len(CHUNKS))] for b in range(NB)]
        slotT_full = sem("slotT_full")
        slotT_hi_ready = sem("slotT_hi_ready")
        slotT_ready = sem("slotT_ready")
        gu_full = sem("gu_full")
        silu_ready = sem("silu_ready")
        h_ready = sem("h_ready")
        hT_full = sem("hT_full")
        hT_ready = sem("hT_ready")
        y_full = sem("y_full")
        y_ready = sem("y_ready")
        dest_ready = sem("dest_ready")
        y_placed = [[sem(f"y_placed{b}_{k}") for k in range(2)] for b in range(NB)]
        gathered = [[sem(f"gathered{b}_{t}") for t in range(0, NT, 2)] for b in range(NB)]
        gates_ready = sem("gates_ready")
        first_added = sem("first_added")
        second_ready = sem("second_ready")
        out_ready = sem("out_ready")
        out_done = sem("out_done")

        def grp(g):
            return slice(g * GT, (g + 1) * GT)

        def cols(g):
            return slice(g * GW, (g + 1) * GW)

        def misc(use):
            return MI[:, MISC[use][0], :]

        def bank_free(use):
            return misc_free[MISC[use][0]]

        def drained(eng, use):
            eng.wait_ge(bank_free(use), MISC[use][1] + 1)

        def wait_misc(eng, use):
            eng.wait_ge(misc_full[MISC[use][0]], MISC[use][1] + 1)

        xg = [x[0, :, :].rearrange("(p t) d -> p t d", t=NT)[:, 0:GT, :],
              x[0, :, :].rearrange("(p t) d -> p t d", t=NT)[:, GT:NT, :],
              x[1, :, :].rearrange("(p t) d -> p t d", t=NT)]
        out_v = out.rearrange("b (p t) d -> p b t d", t=NT)
        xs_tiles = [a.rearrange("(n p) d -> p n d", p=P) for a in xs]
        placed_rows = [a[ST * P:ST * P + K * N, :].rearrange("(k p t) d -> p k t d", k=K, t=NT) for a in placed]

        def load_outputs(eng, b):
            eng.wait_ge(y_placed[b][0], 16 * HALF)
            eng.wait_ge(y_placed[b][1], 16 * (ST - HALF))
            for t in range(0, NT, 2):
                eng.dma_start(rows_of[b][:, :, t:t + 2, :], placed_rows[b][:, :, t:t + 2, :]
                              ).then_inc(gathered[b][t // 2], 16)

        block = ctx.enter_context(nc.Block())

        @block.sync
        def _(sp):
            sp.dma_start(xt[:, 0:GT, :], xg[0]).then_inc(x_in[0], 16)
            sp.dma_start(xt[:, GT:NT, :], xg[1]).then_inc(x_in[1], 16)
            sp.dma_start(xt[:, NT:TILES, :], xg[2]).then_inc(x_in[2], 16)
            for e in range(E):
                if e >= 4:
                    sp.wait_ge(w13_split, e - 3)
                sp.dma_start(stage[:, e % 4, :], w13[:, e, :]).then_inc(w13_in[e % 4], 16)
                if e == 3:
                    sp.dma_start(w2s[:], w2).then_inc(w2_in, 16)
                    sp.wait_ge(zero_ready, 1)
                    for b in range(NB):
                        sp.dma_start(xs[b].rearrange("(n p) d -> p n d", p=P),
                                     zero[:].unsqueeze(1).to_broadcast([P, ST, XR])).then_inc(xs_zeroed[b], 16)

            def load_rows(b):
                drained(sp, ("AV", 2 + b))
                sp.wait_ge(scattered[b], 16 * K * NT)
                for k, (a, z) in enumerate(CHUNKS):
                    sp.dma_start(rows_in[b][:, a:z, :], xs_tiles[b][:, a:z, :]).then_inc(rows_loaded[b][k], 16)

            load_rows(0)
            load_rows(1)
            load_outputs(sp, 0)
            for b in range(NB):
                for t in range(0, NT, 2):
                    sp.wait_ge(out_ready, b * NT + t + 2)
                    sp.dma_start(out_v[:, b, t:t + 2, :], xt[:, b * NT + t:b * NT + t + 2, :]).then_inc(out_done, 16)
            sp.wait_ge(out_done, 16 * NB * NT // 2)

        @block.gpsimd
        def _(pool):
            steps = [0]

            def link(ins):
                steps[0] += 1
                ins.then_inc(pool_step, 1)
                pool.wait_ge(pool_step, steps[0])

            nc.gpsimd.memset(ones[:], 1.0).then_inc(ones_ready, 1)
            nc.gpsimd.memset(zero[:], 0.0).then_inc(zero_ready, 1)
            link(nc.gpsimd.memset(mhalf[:], -0.5))

            def inv_std(n):
                pool.wait_ge(mv_ready, n + 1)
                link(nc.gpsimd.tensor_scalar(rstd[:, grp(n % GROUPS)], mv[:, grp(n % GROUPS), 1], EPS, None, ALU.add))
                nc.gpsimd.tensor_tensor(rstd[:, grp(n % GROUPS)], rstd[:, grp(n % GROUPS)], mhalf[:], ALU.pow).then_inc(rstd_ready, 1)

            inv_std(0)
            inv_std(1)
            pool.wait_ge(w_in, 16)
            link(nc.gpsimd.tensor_copy(wj_hi[:], w[:, W_J:W_J + D]))
            nc.gpsimd.tensor_tensor(wj_lo[:], w[:, W_J:W_J + D], wj_hi[:].bitcast(F32), ALU.subtract).then_inc(wj_ready, 1)

            inv_std(2)
            inv_std(3)
            pool.wait_ge(zero_ready, 1)

            def mean_field(b):
                pool.wait_ge(sT_hi_ready, GB * (b + 1))
                link(nc.gpsimd.tensor_tensor(msum[:], ssum[:, 2 * b:2 * b + 1], ssum[:, 2 * b + 1:2 * b + 2], ALU.add))
                nc.gpsimd.tensor_scalar(meanb[:], zero[:, 0:P], msum[:, 0:1], 1.0 / N,
                                        ALU.add, ALU.mult).then_inc(mean_ready, 1)

            def split_v(q):
                drained(pool, ("V", q))
                link(nc.gpsimd.tensor_copy(v_hi[:, grp(q), :], st[:, grp(q), :]))
                nc.gpsimd.tensor_tensor(v_lo[:, grp(q), :], st[:, grp(q), :], v_hi[:, grp(q), :].bitcast(F32),
                                        ALU.subtract).then_inc(v_ready, 1)

            def add_global(b):
                drained(pool, ("G", b))
                pool.wait_ge(v_ready, GB * (b + 1))
                rows = st[:, b * NT:(b + 1) * NT, :]
                nc.gpsimd.tensor_tensor(rows, rows, gb[:, b, :].unsqueeze(1).to_broadcast([P, NT, D]),
                                        ALU.add).then_inc(sg_ready, 1)

            def split_w13(e):
                pool.wait_ge(w13_in[e % 4], 16 * (e // 4 + 1))
                link(nc.gpsimd.tensor_copy(w13_hi[:, e, :], stage[:, e % 4, :]))
                nc.gpsimd.tensor_tensor(w13_lo[:, e, :], stage[:, e % 4, :], w13_hi[:, e, :].bitcast(F32),
                                        ALU.subtract).then_inc(w13_split, 1)

            def residual(g):
                pool.wait_ge(tanh_ready, g + 1)
                nc.gpsimd.tensor_tensor(xt[:, grp(g), :], xt[:, grp(g), :], arg[:, g % 2, :, :],
                                        ALU.add).then_inc(x1_ready, 1)

            def scatter(b):
                pool.wait_ge(slots_ready, b + 1)
                pool.wait_ge(xs_zeroed[b], 16)
                for t in range(NT):
                    pool.wait_ge(again_ready, GB * b + t // GT + 1)
                    for k in range(K):
                        src = xn_again[b][:, t, :] if k == 1 else xn[:, b * NT + t, :]
                        nc.gpsimd.indirect_dma_start(
                            xs[b][:, :], bass.IndirectOffsetOnAxis(ap=slots[:, b, k, t:t + 1], axis=0),
                            src, None).then_inc(scattered[b], 16)

            def place_outputs(b):
                pool.wait_ge(dest_ready, b + 1)
                for t in range(ST):
                    i = b * ST + t
                    pool.wait_ge(y_ready, i + 1)
                    nc.gpsimd.indirect_dma_start(
                        placed[b][:, :], bass.IndirectOffsetOnAxis(ap=dest[:, i:i + 1], axis=0),
                        y[:, i % Y_PLACES, :], None).then_inc(y_placed[b][t // HALF], 16)

            pool.wait_ge(c_in, 16)
            for b in range(NB):
                link(nc.gpsimd.tensor_copy(xn[:, b * NT:(b + 1) * NT, D], c[:, C_DEST:C_DEST + NT]))
            mean_field(0)
            split_w13(0)
            split_v(0)
            split_v(1)
            add_global(0)
            split_w13(1)
            mean_field(1)
            split_w13(2)
            split_v(2)
            split_v(3)
            add_global(1)
            split_w13(3)
            split_w13(4)
            residual(0)
            inv_std(GROUPS)
            residual(1)
            split_w13(5)
            inv_std(GROUPS + 1)
            split_w13(6)
            split_w13(7)
            scatter(0)
            inv_std(GROUPS + 2)
            inv_std(GROUPS + 3)
            scatter(1)
            for b in range(NB):
                place_outputs(b)

        @block.scalar
        def _(act):
            act.dma_start(c[:], cst).then_inc(c_in, 16)
            act.dma_start(w[:], wpack).then_inc(w_in, 16)
            act.wait_ge(c_in, 16)
            nc.scalar.copy(tri[:], c[:, C_TRI:C_TRI + P]).then_inc(tri_ready, 1)

            def evac_xT(q):
                wait_misc(act, ("xT", q))
                nc.scalar.copy(xnT[:, cols(q)], misc(("xT", q))).then_inc(bank_free(("xT", q)), 1)

            def evac_sT_hi(q):
                wait_misc(act, ("sT", q))
                nc.scalar.activation(sT_hi[:, cols(q)], misc(("sT", q)), ACT.Identity, bias=w[:, B_COL:B_COL + 1],
                                     accum_out=ssum[:, q:q + 1]).then_inc(sT_hi_ready, 1)

            def evac_e_hi(g):
                wait_misc(act, ("e", g))
                nc.scalar.activation(e_hi[:, g % 2, :], misc(("e", g)), ACT.Copy, scale=SCALE).then_inc(e_hi_ready, 1)

            def evac_G(b):
                wait_misc(act, ("G", b))
                nc.scalar.copy(gb[:, b, :], misc(("G", b))[:, 0:D]).then_inc(bank_free(("G", b)), 1)

            def softmax_exp(i):
                act.wait_ge(max_ready, i + 1)
                nc.scalar.activation(probs[:, i % 2, :], S[:, i % 2, :], ACT.Exp, bias=nmax[:, i:i + 1],
                                     accum_out=L[:, i:i + 1]).then_inc(probs_ready, 1)

            def evac_pT_hi(i):
                g, r = divmod(i, GT)
                for k in range(2):
                    act.wait_ge(PT_full, 2 * i + k + 1)
                    nc.scalar.copy(pT_hi[:, g % 2, 4 * k:4 * k + 4, r * P:(r + 1) * P],
                                   PT[:, k, :].rearrange("p (c n) -> p c n", c=4)).then_inc(pT_hi_ready, 1)

            def evac_oT(g):
                wait_misc(act, ("AV", g))
                nc.scalar.copy(oT, misc(("AV", g))).then_inc(bank_free(("AV", g)), 1)

            def tanh(g):
                drained(act, ("OT", g))
                nc.scalar.activation(arg[:, g % 2, :, :], arg[:, g % 2, :, :], ACT.Tanh,
                                     scale=w[:, BETA:BETA + 1]).then_inc(tanh_ready, 1)

            def evac_x2T(g):
                wait_misc(act, ("X2", g))
                nc.scalar.copy(x2T, misc(("X2", g))).then_inc(bank_free(("X2", g)), 1)

            def copy_again(g):
                act.wait_ge(xn_ready, GROUPS + g + 1)
                b, rows = g // GB, slice((g % GB) * GT, (g % GB + 1) * GT)
                nc.scalar.copy(xn_again[b][:, rows, 0:D], xn[:, grp(g), 0:D])
                nc.scalar.copy(xn_again[b][:, rows, D], c[:, C_DEST + NT + rows.start:C_DEST + NT + rows.stop]
                               ).then_inc(again_ready, 1)

            def gate_softmax_exp(b):
                act.wait_ge(gate_sub, b + 1)
                nc.scalar.activation(r64[:, 1, :, :], r64[:, 0, :, :], ACT.Exp).then_inc(gate_exp, 1)

            def evacuate(kind, n):
                if kind == "xT":
                    evac_xT(n)
                elif kind == "sT":
                    evac_sT_hi(n)
                elif kind == "e":
                    evac_e_hi(n)
                elif kind == "G":
                    evac_G(n)
                elif kind == "X2":
                    evac_x2T(n)
                    if 0 < n < 3:
                        copy_again(n)

            act.wait_ge(w_in, 16)
            for kind, n in START[:6]:
                evacuate(kind, n)
            softmax_exp(0)
            evac_G(0)
            for i in range(TILES):
                evac_pT_hi(i)
                for kind, n in BEFORE.get(i, []):
                    evacuate(kind, n)
                if i + 1 < TILES:
                    softmax_exp(i + 1)
                if i == 7:
                    tanh(0)
                if i == 8:
                    tanh(1)
                for kind, n in AFTER.get(i, []):
                    evacuate(kind, n)
                if i == 8:
                    copy_again(0)
                if i in (6, 7, 13):
                    evac_oT({6: 0, 7: 1, 13: 2}[i])
            tanh(2)
            evac_oT(3)

            def silu(t, u):
                act.wait_ge(gu_full, t + 1)
                nc.scalar.activation(sg[:, u, :], S[:, 0, u * 2 * H:u * 2 * H + H], ACT.Silu).then_inc(silu_ready, 1)

            def slotT_hi(t, u):
                act.wait_ge(slotT_full, t + 1)
                nc.scalar.copy(gT_hi[:, u, :], PT[:, 0, u * P:(u + 1) * P]).then_inc(slotT_hi_ready, 1)

            def evac_hT(t, u):
                act.wait_ge(hT_full, t + 1)
                nc.scalar.copy(hT[:, u, :], PT[:, 1, u * H:(u + 1) * H]).then_inc(hT_ready, 1)

            gate_softmax_exp(0)
            tanh(3)
            for kind, n in EARLY:
                evacuate(kind, n)
            slotT_hi(0, 0)
            slotT_hi(1, 1)
            silu(0, 0)
            for kind, n in MIDDLE:
                evacuate(kind, n)
            slotT_hi(2, 0)
            copy_again(3)
            for t in range(PEELED):
                if t >= 1:
                    evac_hT(t - 1, (t - 1) % 2)
                silu(t + 1, (t + 1) % 2)
                slotT_hi(t + 3, (t + 3) % 2)
                for kind, n in LATE.get(t, []):
                    evacuate(kind, n)
            with act.Fori(PEELED // QUAD, SLOT_TILES // QUAD - 1) as r:
                for v in range(QUAD):
                    evac_hT(r * QUAD + v - 1, (v + 1) % 2)
                    silu(r * QUAD + v + 1, (v + 1) % 2)
                    slotT_hi(r * QUAD + v + 3, (v + 1) % 2)
            for t in range(LAST, SLOT_TILES):
                evac_hT(t - 1, (t - 1) % 2)
                if t + 1 < SLOT_TILES:
                    silu(t + 1, (t + 1) % 2)
                if t + 3 < SLOT_TILES:
                    slotT_hi(t + 3, (t + 3) % 2)
            evac_hT(SLOT_TILES - 1, (SLOT_TILES - 1) % 2)
            gate_softmax_exp(1)
            load_outputs(act, 1)
            act.wait_ge(gates_ready, NB)
            act.wait_ge(out_ready, NT)
            for t in range(NT):
                if t % 2 == 0:
                    act.wait_ge(gathered[1][t // 2], 16)
                nc.scalar.activation(second[:, t, :], rows_of[1][:, 1, t, :], ACT.Copy,
                                     scale=gate[:, 1, 1, t:t + 1]).then_inc(second_ready, 1)

        @block.vector
        def _(dve):
            steps = [0]

            def link(ins):
                steps[0] += 1
                ins.then_inc(dve_step, 1)
                dve.wait_ge(dve_step, steps[0])

            def stats(n):
                for j in range(GT):
                    ins = nc.vector.bn_stats(bn[:, n % 2, j, :], xt[:, (n % GROUPS) * GT + j, :])
                link(ins)
                for j in range(GT):
                    ins = nc.vector.bn_aggr(mv[:, (n % GROUPS) * GT + j, :], bn[:, n % 2, j, :])
                ins.then_inc(mv_ready, 1)

            def normalise(n):
                dve.wait_ge(rstd_ready, n + 1)
                for j in range(GT):
                    i = (n % GROUPS) * GT + j
                    ins = nc.vector.tensor_scalar(xn[:, i, 0:D], xt[:, i, :], mv[:, i, 0:1],
                                                  rstd[:, i:i + 1], ALU.subtract, ALU.mult)
                ins.then_inc(xn_ready, 1)

            def evac_sT_lo(q):
                dve.wait_ge(sT_hi_ready, q + 1)
                nc.vector.scalar_tensor_tensor(out=sT_lo[:, cols(q)], in0=misc(("sT", q)), scalar=w[:, B_COL:B_COL + 1],
                                               in1=sT_hi[:, cols(q)].bitcast(F32), op0=ALU.add,
                                               op1=ALU.subtract).then_inc(bank_free(("sT", q)), 1)

            def evac_e_lo(g):
                dve.wait_ge(e_hi_ready, g + 1)
                nc.vector.scalar_tensor_tensor(out=e_lo[:, g % 2, :], in0=misc(("e", g)), scalar=SCALE,
                                               in1=e_hi[:, g % 2, :].bitcast(F32), op0=ALU.mult,
                                               op1=ALU.subtract).then_inc(bank_free(("e", g)), 1)

            def evac_s(q):
                wait_misc(dve, ("V", q))
                ins = nc.vector.tensor_tensor(st[:, grp(q), :], misc(("V", q)).rearrange("p (t d) -> p t d", t=GT),
                                              w[:, B_ROW:B_ROW + D].unsqueeze(1).to_broadcast([P, GT, D]), ALU.add)
                ins.then_inc(bank_free(("V", q)), 1)

            def row_max(i):
                dve.wait_ge(S_full, i + 1)
                nc.vector.tensor_reduce(nmax[:, i:i + 1], S[:, i % 2, :], AXX, ALU.max, negate=True).then_inc(max_ready, 1)

            def evac_pT_lo(i):
                g, r = divmod(i, GT)
                for k in range(2):
                    dve.wait_ge(pT_hi_ready, 2 * i + k + 1)
                    part = (slice(None), g % 2, slice(4 * k, 4 * k + 4), slice(r * P, (r + 1) * P))
                    nc.vector.tensor_tensor(pT_lo[part], PT[:, k, :].rearrange("p (c n) -> p c n", c=4),
                                            pT_hi[part].bitcast(F32), ALU.subtract).then_inc(pT_ready, 1)

            def tanh_arg(g):
                link(nc.vector.reciprocal(L[:, grp(g)], L[:, grp(g)]))
                wait_misc(dve, ("OT", g))
                dve.wait_ge(sg_ready, g // GB + 1)
                for j in range(GT):
                    i = g * GT + j
                    ins = nc.vector.scalar_tensor_tensor(out=arg[:, g % 2, j, :], in0=misc(("OT", g))[:, j * P:(j + 1) * P],
                                                         scalar=L[:, i:i + 1], in1=st[:, i, :], op0=ALU.mult, op1=ALU.add)
                ins.then_inc(bank_free(("OT", g)), 1)

            def residual(g):
                dve.wait_ge(tanh_ready, g + 1)
                link(nc.vector.tensor_tensor(xt[:, grp(g), :], xt[:, grp(g), :], arg[:, g % 2, :, :], ALU.add))

            def stats_after(g):
                dve.wait_ge(x1_ready, g + 1)
                stats(GROUPS + g)

            def take_logits(g):
                wait_misc(dve, ("LG", g))
                nc.vector.tensor_copy(lg[:, grp(g), :], misc(("LG", g))[:, 0:GT * E].rearrange("p (t e) -> p t e", e=E)
                                      ).then_inc(bank_free(("LG", g)), 1)

            def col(n):
                return r8[:, n, :]

            def bc(ap):
                return ap.unsqueeze(2).to_broadcast([P, NT, E])

            def gate_max(b):
                drained(dve, ("LG", GB * b + 1))
                rows = lg[:, b * NT:(b + 1) * NT, :]
                link(nc.vector.tensor_reduce(col(0), rows, AXX, ALU.max))
                nc.vector.tensor_tensor(r64[:, 0, :, :], rows, bc(col(0)), ALU.subtract).then_inc(gate_sub, 1)

            less_max = r64[:, 0, :, :]
            desc = c[:, C_DESC:C_DESC + E].unsqueeze(1).to_broadcast([P, NT, E])

            def choose_first(b):
                dve.wait_ge(gate_sub, b + 1)
                link(nc.vector.scalar_tensor_tensor(out=r64[:, 2, :, :], in0=less_max, scalar=0.0, in1=desc,
                                                    op0=ALU.is_equal, op1=ALU.mult))
                link(nc.vector.tensor_reduce(col(1), r64[:, 2, :, :], AXX, ALU.max))
                link(nc.vector.tensor_tensor(hot[:, 0, :, :], r64[:, 2, :, :], bc(col(1)), ALU.is_equal))

            def choose_second():
                link(nc.vector.scalar_tensor_tensor(out=r64[:, 3, :, :], in0=hot[:, 0, :, :], scalar=-3e38,
                                                    in1=less_max, op0=ALU.mult, op1=ALU.min))
                link(nc.vector.tensor_reduce(col(2), r64[:, 3, :, :], AXX, ALU.max))
                link(nc.vector.tensor_tensor(r64[:, 2, :, :], r64[:, 3, :, :], bc(col(2)), ALU.is_equal))
                link(nc.vector.tensor_tensor(r64[:, 4, :, :], r64[:, 2, :, :], desc, ALU.mult))
                link(nc.vector.tensor_reduce(col(3), r64[:, 4, :, :], AXX, ALU.max))
                link(nc.vector.tensor_tensor(hot[:, 1, :, :], r64[:, 4, :, :], bc(col(3)), ALU.is_equal))
                nc.vector.tensor_tensor(sel[:], hot[:, 0, :, :], hot[:, 1, :, :], ALU.add).then_inc(sel_ready, 1)

            def gate_values(b):
                dve.wait_ge(gate_exp, b + 1)
                ex = r64[:, 1, :, :]
                link(nc.vector.tensor_reduce(col(4), ex, AXX, ALU.add))
                link(nc.vector.reciprocal(col(5), col(4)))
                link(nc.vector.tensor_tensor(prod, hot[:], ex.unsqueeze(1).to_broadcast([P, K, NT, E]), ALU.mult))
                link(nc.vector.tensor_reduce(slotf[:], prod, AXX, ALU.add))
                nc.vector.tensor_tensor(gate[:, b, :, :], slotf[:], col(5).unsqueeze(1).to_broadcast([P, K, NT]),
                                        ALU.mult).then_inc(gates_ready, 1)
                dve.wait_ge(gates_ready, b + 1)

            def place(b):
                wait_misc(dve, ("R", b))
                dve.wait_ge(sg_ready, NB)
                rank = misc(("R", b))[:, 0:NT * E].rearrange("p (t e) -> p t e", e=E)
                count = misc(("R", b))[:, NT * E:NT * E + E]
                full = c[:, C_J:C_J + N // P].unsqueeze(1).to_broadcast([P, E, N // P])
                link(nc.vector.scalar_tensor_tensor(out=cmp[:], in0=full, scalar=float(P),
                                                    in1=count.unsqueeze(2).to_broadcast([P, E, N // P]),
                                                    op0=ALU.mult, op1=ALU.is_lt))
                link(nc.vector.tensor_reduce(tiles_e[:], cmp[:], AXX, ALU.add))
                link(nc.vector.tensor_tensor(cmp[:], tiles_e[:].unsqueeze(1).to_broadcast([P, E, E]),
                                             c[:, C_LT:C_LT + E * E].rearrange("p (e f) -> p e f", f=E), ALU.mult))
                link(nc.vector.tensor_reduce(base[:], cmp[:], AXX, ALU.add))
                nc.vector.scalar_tensor_tensor(out=r64[:, 4, :, :], in0=base[:].unsqueeze(1).to_broadcast([P, NT, E]),
                                               scalar=float(P), in1=rank, op0=ALU.mult,
                                               op1=ALU.add).then_inc(bank_free(("R", b)), 1)
                drained(dve, ("R", b))
                link(nc.vector.tensor_tensor(prod, hot[:], r64[:, 4, :, :].unsqueeze(1).to_broadcast([P, K, NT, E]),
                                             ALU.mult))
                link(nc.vector.tensor_reduce(slotf[:], prod, AXX, ALU.add))
                ins = nc.vector.tensor_scalar(slots[:, b, :, :], slotf[:], float(ST * P - 1), None, ALU.min)
                ins.then_inc(slots_ready, 1)

            def tile_table(b):
                link(nc.vector.tensor_tensor(ends[:], base[:], tiles_e[:], ALU.add))
                link(nc.vector.tensor_tensor(cmpj, ends[0:1, :].unsqueeze(1).to_broadcast([1, ST, E]),
                                             c[0:1, C_J:C_J + ST].unsqueeze(2).to_broadcast([1, ST, E]), ALU.is_le))
                link(nc.vector.tensor_reduce(tabf, cmpj, AXX, ALU.add))
                nc.vector.tensor_scalar(tab[:, b * ST:(b + 1) * ST], tabf, float(E - 1), None,
                                        ALU.min).then_inc(table_ready, 1)

            def combine(t):
                if t % 2 == 0:
                    dve.wait_ge(gathered[0][t // 2], 16)
                for k in range(K):
                    ins = nc.vector.scalar_tensor_tensor(out=xt[:, t, :], in0=rows_of[0][:, k, t, :],
                                                         scalar=gate[:, 0, k, t:t + 1], in1=xt[:, t, :],
                                                         op0=ALU.mult, op1=ALU.add)
                    if k == 0:
                        link(ins)
                ins.then_inc(out_ready, 1)

            def add_first(t):
                dve.wait_ge(gathered[1][t // 2], 16)
                for i in range(t, t + 2):
                    ins = nc.vector.scalar_tensor_tensor(out=xt[:, NT + i, :], in0=rows_of[1][:, 0, i, :],
                                                         scalar=gate[:, 1, 0, i:i + 1], in1=xt[:, NT + i, :],
                                                         op0=ALU.mult, op1=ALU.add)
                ins.then_inc(first_added, 1)

            def add_second(t):
                dve.wait_ge(first_added, t // 2 + 1)
                dve.wait_ge(second_ready, t + 2)
                rows = xt[:, NT + t:NT + t + 2, :]
                nc.vector.tensor_tensor(rows, rows, second[:, t:t + 2, :], ALU.add).then_inc(out_ready, 2)

            for q in range(2):
                dve.wait_ge(x_in[q], 16)
                stats(q)
            normalise(0)
            normalise(1)
            dve.wait_ge(x_in[2], 16)
            stats(2)
            stats(3)
            dve.wait_ge(w_in, 16)

            def evacuate(kind, n):
                if kind == "sT":
                    evac_sT_lo(n)
                elif kind == "e":
                    evac_e_lo(n)
                elif kind == "V":
                    evac_s(n)
                elif kind == "OT":
                    tanh_arg(n)
                elif kind == "LG":
                    take_logits(n)
                    if n % GB == GB - 1:
                        gate_max(n // GB)
                        choose_first(n // GB)
                    if n == GB - 1:
                        choose_second()
                elif kind == "R":
                    place(n)

            for kind, n in START[:6]:
                evacuate(kind, n)
            row_max(0)
            row_max(1)
            evac_s(1)
            normalise(2)
            for i in range(TILES):
                if i != 8:
                    evac_pT_lo(i)
                for kind, n in BEFORE.get(i, []):
                    evacuate(kind, n)
                if i == 8:
                    normalise(GROUPS)
                    evac_pT_lo(i)
                if i + 2 < TILES and i != 11:
                    row_max(i + 2)
                for kind, n in AFTER.get(i, []):
                    evacuate(kind, n)
                if i == 11:
                    row_max(i + 2)
                if i == 0:
                    normalise(3)
                if i in (7, 8):
                    stats_after(i - 7)
                if i == 9:
                    normalise(GROUPS + 1)
            residual(2)
            stats(GROUPS + 2)
            tile_table(0)

            def hidden(t, u):
                dve.wait_ge(silu_ready, t + 1)
                nc.vector.tensor_tensor(h[:, u, :], sg[:, u, :], S[:, 0, u * 2 * H + H:(u + 1) * 2 * H],
                                        ALU.mult).then_inc(h_ready, 1)

            def slotT_lo(t, u):
                dve.wait_ge(slotT_hi_ready, t + 1)
                nc.vector.tensor_tensor(gT_lo[:, u, :], PT[:, 0, u * P:(u + 1) * P], gT_hi[:, u, :].bitcast(F32),
                                        ALU.subtract).then_inc(slotT_ready, 1)

            def evac_y(t, u, place):
                dve.wait_ge(y_full, t + 1)
                nc.vector.tensor_copy(y[:, bass.ds(place, 1), :].rearrange("p a d -> p (a d)"),
                                      S[:, 1, u * GW:u * GW + D]).then_inc(y_ready, 1)

            tanh_arg(3)
            gate_values(0)
            normalise(GROUPS + 2)
            residual(3)
            stats(GROUPS + 3)
            take_logits(2)
            slotT_lo(0, 0)
            slotT_lo(1, 1)
            normalise(GROUPS + 3)
            slotT_lo(2, 0)
            hidden(0, 0)
            for t in range(PEELED):
                if t >= 2:
                    evac_y(t - 2, t % 2, t - 2)
                hidden(t + 1, (t + 1) % 2)
                slotT_lo(t + 3, (t + 1) % 2)
                for kind, n in LATE.get(t, []):
                    evacuate(kind, n)
                    if kind == "R":
                        tile_table(n)
                if t == 1:
                    choose_second()

            def loop(first, end, first_place):
                with dve.Fori(first // QUAD, end // QUAD) as r:
                    for v in range(QUAD):
                        evac_y(r * QUAD + v - 2, v % 2, r * QUAD + v - first + first_place)
                        hidden(r * QUAD + v + 1, (v + 1) % 2)
                        slotT_lo(r * QUAD + v + 3, (v + 1) % 2)

            def output_rows(b):
                for k in range(len(CHUNKS)):
                    dve.wait_ge(rows_loaded[b][k], 16)
                nc.vector.tensor_tensor(dest[:, b * ST:(b + 1) * ST], rows_in[b][:, :, D], c[:, C_EMPTY:C_EMPTY + ST],
                                        ALU.max).then_inc(dest_ready, 1)

            output_rows(0)
            loop(PEELED, Y_PLACES + 2, PEELED - 2)
            output_rows(1)
            dve.wait_ge(y_placed[0][0], 16 * HALF)
            loop(Y_PLACES + 2, LAST, 0)
            dve.wait_ge(y_placed[0][1], 16 * (ST - HALF))
            for t in range(LAST, SLOT_TILES):
                evac_y(t - 2, t % 2, t - 2 - Y_PLACES)
                if t + 1 < SLOT_TILES:
                    hidden(t + 1, (t + 1) % 2)
                if t + 3 < SLOT_TILES:
                    slotT_lo(t + 3, (t + 3) % 2)
                combine(t - LAST)
            for t in range(SLOT_TILES - 2, SLOT_TILES):
                evac_y(t, t % 2, t - Y_PLACES)
            for t in range(SLOT_TILES - LAST, NT):
                combine(t)
            gate_values(1)
            for t in range(0, NT + 2, 2):
                if t < NT:
                    add_first(t)
                if t > 0:
                    add_second(t - 2)

        @block.tensor
        def _(pe):
            def take(use):
                k, turn = MISC[use]
                if turn > 0:
                    pe.wait_ge(misc_free[k], turn)

            def matmul3(dst, w_hi, w_lo, m_hi, m_lo, start, stop):
                pe.matmul(dst, w_hi, m_hi, start=start, stop=False)
                pe.matmul(dst, w_hi, m_lo, start=False, stop=False)
                return pe.matmul(dst, w_lo, m_hi, start=False, stop=stop)

            def transposes(use, src):
                take(use)
                for j in range(GT):
                    ins = pe.transpose(misc(use)[:, j * P:(j + 1) * P], src(j), ident)
                ins.then_inc(misc_full[MISC[use][0]], 1)

            def xT(q):
                pe.wait_ge(xn_ready, q + 1)
                transposes(("xT", q), lambda j: xn[:, q * GT + j, 0:D])

            def sT(q):
                use = ("sT", q)
                take(use)
                drained(pe, ("xT", q))
                pe.matmul(misc(use), w[:, W_SPIN:W_SPIN + D], xnT[:, cols(q)], start=True,
                          stop=True).then_inc(misc_full[MISC[use][0]], 1)

            def V(q):
                use = ("V", q)
                take(use)
                for j in range(GT):
                    i = q * GT + j
                    ins = pe.matmul(misc(use)[:, j * P:(j + 1) * P], xnT[:, i * P:(i + 1) * P],
                                    w[:, W_SPIN:W_SPIN + D], start=True, stop=True)
                ins.then_inc(misc_full[MISC[use][0]], 1)

            def G(b):
                use = ("G", b)
                take(use)
                pe.wait_ge(mean_ready, b + 1)
                pe.matmul(misc(use)[:, 0:D], meanb[:], w[:, W_GLOB:W_GLOB + D], start=True,
                          stop=True).then_inc(misc_full[MISC[use][0]], 1)

            def energies(g):
                use = ("e", g)
                take(use)
                if g == 0:
                    pe.wait_ge(wj_ready, 1)
                drained(pe, ("sT", g))
                matmul3(misc(use), wj_hi[:], wj_lo[:], sT_hi[:, cols(g)], sT_lo[:, cols(g)], True,
                        True).then_inc(misc_full[MISC[use][0]], 1)

            def scores_of(i):
                g, r = divmod(i, GT)
                b = i // NT
                if r == 0:
                    drained(pe, ("e", g))
                q = slice(r * P, (r + 1) * P)
                for k in range(GB):
                    ins = matmul3(S[:, i % 2, k * GW:(k + 1) * GW], e_hi[:, g % 2, q], e_lo[:, g % 2, q],
                                  sT_hi[:, cols(GB * b + k)], sT_lo[:, cols(GB * b + k)], True, True)
                ins.then_inc(S_full, 1)

            def transpose_probs(i):
                pe.wait_ge(probs_ready, i + 1)
                for k in range(2):
                    if i > 0:
                        pe.wait_ge(pT_ready, 2 * (i - 1) + k + 1)
                    for m in range(4):
                        ch = 4 * k + m
                        ins = pe.transpose(PT[:, k, m * P:(m + 1) * P], probs[:, i % 2, ch * P:(ch + 1) * P], ident)
                    ins.then_inc(PT_full, 1)

            def AV(g, share):
                use = ("AV", g)
                b = g // GB
                half, part = divmod(share, SHARES // 2)
                if share == 0:
                    take(use)
                    pe.wait_ge(v_ready, GB * (b + 1))
                if part == 0:
                    pe.wait_ge(pT_ready, 2 * (GT * g + (half + 1) * GT // 2))
                q = slice(half * GW // 2, (half + 1) * GW // 2)
                for ch in range(part * 2 * CH // SHARES, (part + 1) * 2 * CH // SHARES):
                    i = b * NT + ch
                    ins = matmul3(misc(use)[:, q], v_hi[:, i, :], v_lo[:, i, :], pT_hi[:, g % 2, ch, q],
                                  pT_lo[:, g % 2, ch, q], ch == 0, ch == CH - 1)
                if share == SHARES - 1:
                    ins.then_inc(misc_full[MISC[use][0]], 1)

            def OT(g):
                drained(pe, ("AV", g))
                transposes(("OT", g), lambda j: oT[:, j * P:(j + 1) * P])

            def X2(g):
                pe.wait_ge(xn_ready, GROUPS + g + 1)
                transposes(("X2", g), lambda j: xn[:, g * GT + j, 0:D])

            def LG(g):
                use = ("LG", g)
                take(use)
                drained(pe, ("X2", g))
                for j in range(GT):
                    ins = pe.matmul(misc(use)[:, j * E:(j + 1) * E], x2T[:, j * P:(j + 1) * P],
                                    w[:, W_GATE:W_GATE + E], start=True, stop=True)
                ins.then_inc(misc_full[MISC[use][0]], 1)

            def R(b):
                use = ("R", b)
                take(use)
                pe.wait_ge(sel_ready, b + 1)
                bank = misc(use)
                rank = bank[:, 0:NT * E].rearrange("p (t e) -> p t e", e=E)
                pe.matmul(rank, tri[:], sel[:], start=True, stop=True, skip_group_check=True)
                for t in range(NT - 1):
                    pe.matmul(rank[:, t + 1:NT, :], ones[:], sel[:, t:t + 1, :].to_broadcast([P, NT - 1 - t, E]),
                              start=False, stop=True, skip_group_check=True)
                for t in range(NT):
                    ins = pe.matmul(bank[:, NT * E:NT * E + E], ones[:], sel[:, t, :], start=(t == 0),
                                    stop=(t == NT - 1))
                ins.then_inc(misc_full[MISC[use][0]], 1)

            def keep_busy(times):
                for _ in range(times):
                    pe.matmul(PT[:, 0, :], ones[:], ones[:].unsqueeze(1).to_broadcast([P, GT, P]), start=True, stop=True)

            pe.wait_ge(ones_ready, 1)
            keep_busy(WARM_UP)
            pe.wait_ge(c_in, 16)
            pe.wait_ge(w_in, 16)
            shares_done = {g: 0 for g in range(GROUPS)}

            def do(kind, n):
                if kind == "AV":
                    AV(n, shares_done[n])
                    shares_done[n] += 1
                else:
                    {"xT": xT, "sT": sT, "e": energies, "V": V, "G": G, "OT": OT, "X2": X2, "LG": LG, "R": R}[kind](n)

            for kind, n in START[:6]:
                do(kind, n)
            scores_of(0)
            scores_of(1)
            for kind, n in START[6:]:
                do(kind, n)
            pe.wait_ge(tri_ready, 1)
            for i in range(TILES):
                transpose_probs(i)
                for kind, n in BEFORE.get(i, []):
                    do(kind, n)
                if i + 2 < TILES:
                    scores_of(i + 2)
                for kind, n in AFTER.get(i, []):
                    do(kind, n)
            def experts_of(first, n):
                _, e = nc.values_load_multi_w_load_instructions(
                    tab[0:1, bass.ds(first, n)], engines=[mybir.EngineType.PE], min_val=0, max_val=E - 1,
                    skip_runtime_bounds_check_because="the table is cut off at the last expert")
                return e

            def slotT(t):
                if t > 0:
                    pe.wait_ge(slotT_ready, t)
                pe.transpose(PT[:, 0, (t % 2) * P:(t % 2 + 1) * P], rows_in[t // ST][:, t % ST, 0:D], ident
                             ).then_inc(slotT_full, 1)

            def rows_there(t):
                for k, (a, z) in enumerate(CHUNKS):
                    if t % ST == a:
                        pe.wait_ge(rows_loaded[t // ST][k], 16)

            def gate_up(t, u, e, taken):
                pe.wait_ge(slotT_ready, t + 1)
                if taken is not None:
                    pe.wait_ge(h_ready, taken)
                bank = S[:, 0, u * 2 * H:(u + 1) * 2 * H]
                hi, lo = [a[:, bass.ds(e, 1), :].rearrange("p a n -> p (a n)") for a in (w13_hi, w13_lo)]
                pe.matmul(bank, gT_hi[:, u, :], hi, start=True, stop=False)
                pe.matmul(bank, gT_lo[:, u, :], hi, start=False, stop=False)
                pe.matmul(bank, gT_hi[:, u, :], lo, start=False, stop=True).then_inc(gu_full, 1)

            def hiddenT(t, u):
                pe.wait_ge(h_ready, t + 1)
                for k in range(2):
                    ins = pe.transpose(PT[:, 1, u * H + k * P:u * H + (k + 1) * P], h[:, u, k * P:(k + 1) * P], ident)
                ins.then_inc(hT_full, 1)

            def down(t, u, e, taken):
                pe.wait_ge(hT_ready, t + 1)
                if taken is not None:
                    pe.wait_ge(y_ready, taken)
                for k in range(2):
                    ins = pe.matmul(S[:, 1, u * GW:u * GW + D], hT[:, u, k * P:(k + 1) * P],
                                    w2s[:, bass.ds(e, 1), k, :].rearrange("p a n -> p (a n)"), start=(k == 0), stop=(k == 1))
                ins.then_inc(y_full, 1)

            for kind, n in EARLY:
                do(kind, n)
                if kind == "OT":
                    keep_busy(STAY_WARM)
            pe.wait_ge(w13_split, E)
            pe.wait_ge(w2_in, 16)
            rows_there(0)
            pe.wait_ge(table_ready, 1)
            ex = experts_of(0, BATCH + 1)
            slotT(0)
            slotT(1)
            gate_up(0, 0, ex[0], None)
            for kind, n in MIDDLE:
                do(kind, n)
            slotT(2)
            for t in range(SLOT_TILES):
                if t % BATCH == 0 and t > 0:
                    pe.wait_ge(table_ready, min((t + BATCH) // ST + 1, NB))
                    ex = list(ex[-3:]) + list(experts_of(t + 1, min(BATCH, SLOT_TILES - t - 1)))
                base_t = max(t // BATCH * BATCH - 2, 0)
                if t >= 2:
                    down(t - 2, t % 2, ex[t - 2 - base_t], t - 3 if t > 3 else None)
                if t >= 1:
                    hiddenT(t - 1, (t - 1) % 2)
                if t + 1 < SLOT_TILES:
                    gate_up(t + 1, (t + 1) % 2, ex[t + 1 - base_t], t if t >= 1 else None)
                if t + 3 < SLOT_TILES:
                    rows_there(t + 3)
                    slotT(t + 3)
                for kind, n in LATE.get(t, []):
                    do(kind, n)
            down(SLOT_TILES - 2, 0, ex[-2], SLOT_TILES - 3)
            hiddenT(SLOT_TILES - 1, 1)
            down(SLOT_TILES - 1, 1, ex[-1], SLOT_TILES - 2)


def kernel(L0_attn_x, L0_attn_W_spin, L0_attn_b_spin, L0_attn_W_global, L0_attn_W_J, L0_attn_beta,
           L0_ffn_gate_w, L0_ffn_w1, L0_ffn_w2, L0_ffn_w3):
    import concourse.bacc as bacc
    from concourse.bass_utils import run_bass_kernel_spmd

    b = np.asarray(L0_attn_b_spin)
    wpack = np.concatenate([
        np.asarray(L0_attn_W_spin).T, np.asarray(L0_attn_W_J).T, np.asarray(L0_attn_W_global).T,
        np.broadcast_to(b[None, :], (P, D)), np.asarray(L0_ffn_gate_w).T, b[:, None],
        np.broadcast_to(np.asarray(L0_attn_beta)[None, :], (P, 1))], axis=1)
    w13 = np.concatenate([np.asarray(L0_ffn_w1), np.asarray(L0_ffn_w3)], axis=2).transpose(1, 0, 2)
    w2 = np.asarray(L0_ffn_w2).reshape(E, 2, P, D).transpose(2, 0, 1, 3)
    arrays = {"x": np.asarray(L0_attn_x), "wpack": wpack, "cst": constants(), "w13": w13, "w2": w2}
    arrays = {k: np.ascontiguousarray(v) for k, v in arrays.items()}

    nc = bacc.Bacc("TRN2", target_bir_lowering=False, num_devices=1)
    ins = [nc.dram_tensor(k, v.shape, F32, kind="ExternalInput").ap() for k, v in arrays.items()]
    xs = [nc.dram_tensor(f"xs{i}", (ST * P, XR), F32).ap() for i in range(NB)]
    placed = [nc.dram_tensor(f"placed{i}", (ST * P + K * N, D), F32).ap() for i in range(NB)]
    out = nc.dram_tensor("out", (NB, N, D), F32, kind="ExternalOutput").ap()
    build(nc, *ins, xs, placed, out)
    r = run_bass_kernel_spmd(nc, [arrays], core_ids=[0])
    return r.results[0]["out"]
```
